# Optimizing a Trainium2 kernel written in Bass

```python
import numpy as np
import jax
import jax.numpy as jnp

def _softmax(x, axis=-1):
    return jax.nn.softmax(x, axis=axis)

def _gelu(x):
    return jax.nn.gelu(x, approximate=True)

def _silu(x):
    return jax.nn.silu(x)

def _sigmoid(x):
    return jax.nn.sigmoid(x)

def _layernorm(x, axis=-1, eps=1e-05):
    m = jnp.mean(x, axis=axis, keepdims=True)
    v = jnp.var(x, axis=axis, keepdims=True)
    return (x - m) / jnp.sqrt(v + eps)

def _scatter_add(tgt, idx, src, axis=0):
    return tgt.at[idx].add(src)

def _segment_sum(src, seg, n):
    return jax.ops.segment_sum(src, seg, n)
kernel_name = 'mk_adaln_ffn_d2_seqx_r4_f29fa9'

def setup_inputs(seed: int=0):
    np.random.seed(seed)
    _w = jnp.asarray

    def _rec_inputs():
        import jax
        import jax.numpy as jnp
        _rk = jax.random.key(seed)
        x = -7.109e-05 + 0.9999 * jax.random.normal(jax.random.fold_in(_rk, 1), (8, 256, 1024), jnp.float32)
        _lenS = 256 - jax.random.randint(jax.random.fold_in(_rk, 7), (8,), 0, max(1, 256 // 4) + 1, jnp.int32)
        _lenS2 = 256 - jax.random.randint(jax.random.fold_in(_rk, 8), (8,), 0, max(1, 256 // 4) + 1, jnp.int32)
        condB_thresholds = jax.random.uniform(jax.random.fold_in(_rk, 11), (8,), jnp.float32, 0.0, 1.82799)
        condB_deltas = jax.random.uniform(jax.random.fold_in(_rk, 12), (8,), jnp.float32, 0.0, 0.0232459)
        condB_zeropoints = jax.random.uniform(jax.random.fold_in(_rk, 13), (8,), jnp.float32, 0.0, 243)
        itok_B_0_2 = jax.random.randint(jax.random.fold_in(_rk, 14), (8,), 0, 3, jnp.int32)
        return (x, condB_thresholds, condB_deltas, condB_zeropoints, itok_B_0_2)
    x, condB_thresholds, condB_deltas, condB_zeropoints, itok_B_0_2 = _rec_inputs()

    def _L0_cond_setup():
        import jax, jax.numpy as jnp
        import numpy as np
        N_LEVELS = 64
        key = jax.random.key(seed)
        k1, k2, k3, k4 = jax.random.split(key, 4)
        x = jax.random.normal(k1, (4, 1024, 1024), dtype=jnp.float32)
        G = 4
        thresholds = jnp.sort(jax.random.uniform(k2, (G,), minval=0.2, maxval=3.0))[::-1].astype(jnp.float32)
        deltas = (jax.random.uniform(k3, (G,)) * 0.02 + 0.005).astype(jnp.float32)
        zero_points = jnp.round(jax.random.uniform(k4, (G,)) * (N_LEVELS - 1)).astype(jnp.float32)
        return {'x': x, 'thresholds': thresholds, 'deltas': deltas, 'zero_points': zero_points}
    _L0_cond_all = _L0_cond_setup()
    _L0_cond_in = {k: v for k, v in _L0_cond_all.items() if k in ()}
    del _L0_cond_all

    def _L0_ffn_setup():
        import jax, jax.numpy as jnp
        import numpy as np
        LORA_SCALE = 16.0 / jnp.sqrt(16.0)
        TOP_K = 2
        key = jax.random.key(seed)
        k1, k2, k3, k4 = jax.random.split(key, 4)
        B_, S, D, O, E, R = (4, 512, 1024, 1024, 4, 16)
        x = jax.random.normal(k1, (B_, S, D), dtype=jnp.float32)
        router_w = jax.random.normal(k2, (E, D), dtype=jnp.float32) * 0.02
        A = jax.random.normal(k3, (E, R, D), dtype=jnp.float32) * 0.02
        B = jax.random.normal(k4, (O,), dtype=jnp.float32)
        B = jax.random.normal(k4, (E, O, R), dtype=jnp.float32) * 0.02
        return {'x': x, 'router_w': router_w, 'A': A, 'B': B}
    _L0_ffn_all = _L0_ffn_setup()
    _L0_ffn_in = {k: v for k, v in _L0_ffn_all.items() if k in ('router_w', 'A', 'B')}
    del _L0_ffn_all

    def _L1_cond_setup():
        import jax, jax.numpy as jnp
        import numpy as np
        B, S, D_IN, D_OUT = (4, 512, 1024, 1024)
        R, NUM_LABELERS = (32, 5)
        LORA_SCALING = 16 / 32
        key = jax.random.key(seed)
        k1, k2, k3, k4, k5 = jax.random.split(key, 5)
        x = jax.random.normal(k1, (B, S, D_IN), dtype=jnp.float32)
        labeler_index = jax.random.randint(k2, (B,), 0, NUM_LABELERS, dtype=jnp.int64)
        W = jax.random.normal(k3, (D_OUT, D_IN), dtype=jnp.float32) * 0.02
        lora_A = jax.random.normal(k4, (NUM_LABELERS, D_IN, R), dtype=jnp.float32) * 0.02
        lora_B_w = jax.random.normal(k5, (D_OUT, R), dtype=jnp.float32) * 0.02
        return {'x': x, 'labeler_index': labeler_index, 'W': W, 'lora_A': lora_A, 'lora_B_w': lora_B_w}
    _L1_cond_all = _L1_cond_setup()
    _L1_cond_in = {k: v for k, v in _L1_cond_all.items() if k in ('W', 'lora_A', 'lora_B_w')}
    del _L1_cond_all

    def _L1_ffn_setup():
        import jax, jax.numpy as jnp
        import numpy as np
        B, T, D_IN, D_OUT = (8, 512, 1024, 1024)
        N_LORAS, RANK = (16, 32)
        SCALING = 1.0
        key = jax.random.key(seed)
        ks = jax.random.split(key, 8)
        std = 1.0 / D_IN ** 0.5
        x = jax.random.normal(ks[0], (B, T, D_IN), dtype=jnp.float32)
        idx = jax.random.randint(ks[1], (B,), 0, N_LORAS)
        gate = jax.nn.one_hot(idx, N_LORAS, dtype=jnp.float32)
        kernel = jax.random.normal(ks[2], (D_IN, D_OUT), dtype=jnp.float32) * std
        bias = jnp.zeros((D_OUT,), dtype=jnp.float32)
        lora_A = jax.random.normal(ks[3], (N_LORAS, RANK, D_IN), dtype=jnp.float32) * std
        lora_B = jax.random.normal(ks[4], (N_LORAS, D_OUT, RANK), dtype=jnp.float32) * 0.01
        lora_A_shared = jax.random.normal(ks[5], (RANK, D_IN), dtype=jnp.float32) * std
        lora_B_shared = jax.random.normal(ks[6], (D_OUT, RANK), dtype=jnp.float32) * 0.01
        return {'x': x, 'gate': gate, 'kernel': kernel, 'bias': bias, 'lora_A': lora_A, 'lora_B': lora_B, 'lora_A_shared': lora_A_shared, 'lora_B_shared': lora_B_shared}
    _L1_ffn_all = _L1_ffn_setup()
    _L1_ffn_in = {k: v for k, v in _L1_ffn_all.items() if k in ('gate', 'kernel', 'bias', 'lora_A', 'lora_B', 'lora_A_shared', 'lora_B_shared')}
    del _L1_ffn_all
    return {'x': x, 'condB_thresholds': condB_thresholds, 'condB_deltas': condB_deltas, 'condB_zeropoints': condB_zeropoints, 'itok_B_0_2': itok_B_0_2, 'L0_ffn_router_w': _L0_ffn_in['router_w'], 'L0_ffn_A': _L0_ffn_in['A'], 'L0_ffn_B': _L0_ffn_in['B'], 'L1_cond_W': _L1_cond_in['W'], 'L1_cond_lora_A': _L1_cond_in['lora_A'], 'L1_cond_lora_B_w': _L1_cond_in['lora_B_w'], 'L1_ffn_gate': _L1_ffn_in['gate'], 'L1_ffn_kernel': _L1_ffn_in['kernel'], 'L1_ffn_bias': _L1_ffn_in['bias'], 'L1_ffn_lora_A': _L1_ffn_in['lora_A'], 'L1_ffn_lora_B': _L1_ffn_in['lora_B'], 'L1_ffn_lora_A_shared': _L1_ffn_in['lora_A_shared'], 'L1_ffn_lora_B_shared': _L1_ffn_in['lora_B_shared']}

def reference(x, condB_thresholds, condB_deltas, condB_zeropoints, itok_B_0_2, L0_ffn_router_w, L0_ffn_A, L0_ffn_B, L1_cond_W, L1_cond_lora_A, L1_cond_lora_B_w, L1_ffn_gate, L1_ffn_kernel, L1_ffn_bias, L1_ffn_lora_A, L1_ffn_lora_B, L1_ffn_lora_A_shared, L1_ffn_lora_B_shared):
    import jax
    import jax.numpy as jnp

    def _L0_cond_ref(x, thresholds, deltas, zero_points):
        import jax, jax.numpy as jnp
        import numpy as np
        N_LEVELS = 64
        G = thresholds.shape[0]
        gi = jnp.sum(jnp.abs(x)[..., None] <= thresholds, axis=-1)
        idx = jnp.minimum(gi, G - 1)
        d = deltas[idx]
        zp = zero_points[idx]
        x_quant = jnp.clip(jnp.round(x / d) + zp, 0, N_LEVELS - 1)
        x_dequant = (x_quant - zp) * d
        return jnp.where(gi == G, jnp.float32(0), x_dequant)

    def _L0_ffn_ref(x, router_w, A, B):
        import jax, jax.numpy as jnp
        import numpy as np
        LORA_SCALE = 16.0 / jnp.sqrt(16.0)
        TOP_K = 2
        D = x.shape[-1]
        flat = x.reshape(-1, D)
        logits = flat @ router_w.T
        topk_vals, topk_idx = jax.lax.top_k(logits, TOP_K)
        sparse = jnp.full_like(logits, -jnp.inf)
        rows = jnp.arange(logits.shape[0])[:, None]
        sparse = sparse.at[rows, topk_idx].set(topk_vals)
        gates = jax.nn.softmax(sparse, axis=-1)
        mid = jnp.einsum('tf,erf->ter', flat, A)
        all_deltas = jnp.einsum('ter,eor->teo', mid, B) * LORA_SCALE
        delta = jnp.einsum('te,teo->to', gates, all_deltas)
        return delta.reshape(*x.shape[:-1], -1)

    def _L1_cond_ref(x, labeler_index, W, lora_A, lora_B_w):
        import jax, jax.numpy as jnp
        import numpy as np
        B, S, D_IN, D_OUT = (4, 512, 1024, 1024)
        R, NUM_LABELERS = (32, 5)
        LORA_SCALING = 16 / 32
        base = jnp.einsum('bsi,oi->bso', x, W)
        labelers_A = lora_A[labeler_index]
        low = jnp.einsum('bsi,bir->bsr', x, labelers_A)
        delta = jnp.einsum('bsr,or->bso', low, lora_B_w) * LORA_SCALING
        return base + delta

    def _L1_ffn_ref(x, gate, kernel, bias, lora_A, lora_B, lora_A_shared, lora_B_shared):
        import jax, jax.numpy as jnp
        import numpy as np
        B, T, D_IN, D_OUT = (8, 512, 1024, 1024)
        N_LORAS, RANK = (16, 32)
        SCALING = 1.0
        base_out = jnp.matmul(x, kernel) + bias
        b = gate.shape[0]
        x_flat = x.reshape(b, -1, x.shape[-1])
        A_eff = jnp.einsum('bn,nri->bri', gate, lora_A)
        B_eff = jnp.einsum('bn,nor->bor', gate, lora_B)
        Ax = jnp.einsum('bri,bti->btr', A_eff, x_flat)
        delta_flat = jnp.einsum('bor,btr->bto', B_eff, Ax)
        Ax_s = jnp.einsum('ri,bti->btr', lora_A_shared, x_flat)
        delta_flat = delta_flat + jnp.einsum('or,btr->bto', lora_B_shared, Ax_s)
        delta = delta_flat.reshape(x.shape[:-1] + (kernel.shape[-1],))
        return base_out + (SCALING * delta).astype(base_out.dtype)
    x = x + _L0_ffn_ref(_L0_cond_ref(x, condB_thresholds, condB_deltas, condB_zeropoints), L0_ffn_router_w, L0_ffn_A, L0_ffn_B)
    x = x + _L1_ffn_ref(_L1_cond_ref(x, itok_B_0_2, L1_cond_W, L1_cond_lora_A, L1_cond_lora_B_w), L1_ffn_gate, L1_ffn_kernel, L1_ffn_bias, L1_ffn_lora_A, L1_ffn_lora_B, L1_ffn_lora_A_shared, L1_ffn_lora_B_shared)
    return x

_drawn_inputs = setup_inputs


def setup_inputs(seed=0):
    import zlib

    import numpy as np

    out = dict(_drawn_inputs(seed))
    spreads = {'L1_ffn_bias': (0.0, 0.1)}
    factors = {'L1_cond_lora_A': 2.748,
     'L1_cond_lora_B_w': 2.745,
     'L1_ffn_lora_A': 2.753,
     'L1_ffn_lora_B': 2.755,
     'L1_ffn_lora_A_shared': 2.772,
     'L1_ffn_lora_B_shared': 2.782}
    for name, (base, spread) in spreads.items():
        noise = np.random.default_rng([zlib.crc32(name.encode()), seed]).standard_normal(out[name].shape)
        drawn = base * np.exp(spread * noise) if base else spread * noise
        out[name] = jnp.asarray(drawn.astype(out[name].dtype))
    for name, factor in factors.items():
        out[name] = (out[name] * factor).astype(out[name].dtype)
    return out
```

```python
import numpy as np
import concourse.bass as bass
from concourse import mybir

F32 = mybir.dt.float32
F32R = mybir.dt.float32r
I16 = mybir.dt.int16
I32 = mybir.dt.int32
U8 = mybir.dt.uint8
ALU = mybir.AluOpType
ACT = mybir.ActivationFunctionType
AX = mybir.AxisListType.X

P = 128
BATCH = 8
TOK = 256
TT = TOK // P
D = 1024
KT = D // P
G = 8
E, R0 = 4, 16
ER = E * R0
RT = ER + E
R = 32
NL = 16
RG = P // NL
NG = R // RG
LAB = 5
HALF = D // 2
HALVES = 2
STEPS = HALVES * KT
BG = P // R
LEVELS = 63.0
TOP_K = 2.0
LORA0 = 4.0
LORA1 = 0.5


def build(nc, a, out_t, itok):
    arena = [(nc.sbuf_base + 31) // 32 * 32]

    def place(name, shape, dt, at=None, after=0):
        size = int(np.prod(shape[1:])) * mybir.dt.size(dt)
        size = (size + 31) // 32 * 32
        if at is None:
            at = arena[0]
            arena[0] += size
        t = nc.alloc_sbuf_tensor_at(name, shape, dt, offset=at + after)
        return t[:], at

    p_hi, _ = place("p_hi", [P, HALVES, KT, HALF], F32R)
    p_lo, p_lo_at = place("p_lo", [P, HALVES, KT, HALF], F32R)
    p_hi_at = p_lo_at - HALVES * KT * HALF * 4
    half_bytes = KT * HALF * 4
    val, _ = place("val", [P, 3, KT, TOK], F32)
    absx, _ = place("absx", [P, KT, TOK], F32)
    level, _ = place("level", [P, 2, KT, TOK], I16)
    inside, _ = place("inside", [P, 2, KT, TOK], U8)
    xq, _ = place("xq", [P, 2, KT, TOK], F32)
    xbuf, xbuf_at = place("xbuf", [P, 2, KT, TOK], F32)
    x1_hi, x1_at = place("x1_hi", [P, 2, KT, TOK], F32R)
    x1_lo, x1_lo_at = place("x1_lo", [P, 2, KT, TOK], F32R)
    ub, ub_at = place("ub", [P, 2, KT, 2 * R], F32)
    tb, tb_at = place("tb", [2 * R, 2, D], F32)
    uall, _ = place("uall", [P, BATCH, KT, R], F32)
    ra, _ = place("ra", [P, KT, RT], F32)
    ber, _ = place("ber", [ER, D], F32)
    mg, _ = place("mg", [P, TT, ER], F32)
    mgt, mgt_at = place("mgt", [ER, TOK], F32)
    zt, _ = place("zt", [2 * R, TOK], F32)
    ident, _ = place("ident", [P, P], F32)
    bias, _ = place("bias", [P, KT], F32)
    par, _ = place("par", [P, 3, G], F32)
    thr, _ = place("thr", [P, G], F32)
    inv, _ = place("inv", [P, G], F32)
    shift, _ = place("shift", [P, G], F32)
    unshift, _ = place("unshift", [P, G], F32)
    width, _ = place("width", [P, G], F32)
    before, _ = place("before", [P, TT, E, E], F32)
    lg, _ = place("lg", [P, TT, E], F32)
    beats, _ = place("beats", [P, TT, E, E], F32)
    ties, _ = place("ties", [P, TT, E, E], F32)
    rank, _ = place("rank", [P, TT, E], F32)
    best, _ = place("best", [P, TT], F32)
    gap, _ = place("gap", [P, TT, E], F32)
    expo, _ = place("expo", [P, TT, E], F32)
    gates, _ = place("gates", [P, TT, E], F32)
    total, _ = place("total", [P, TT], F32)
    idle, _ = place("idle", [P, 1], F32)
    itok_sb, _ = place("itok_sb", [1, BATCH], I32)
    gate_rep, _ = place("gate_rep", [P, BATCH], F32)
    gsel, _ = place("gsel", [P, RG], F32)
    gmix, _ = place("gmix", [P, BATCH, RG], F32)
    kp_hi, _ = place("kp_hi", [P, KT, HALF], F32R, xbuf_at)
    la, _ = place("la", [P, NG, D], F32, xbuf_at)
    kp_lo, _ = place("kp_lo", [P, KT, HALF], F32R, x1_at)
    lb, _ = place("lb", [P, NG, D], F32, x1_at)
    w_hi, _ = place("w_hi", [P, 2, KT, P], F32R, x1_lo_at)
    w_lo, _ = place("w_lo", [P, 2, KT, P], F32R, x1_lo_at, 2 * KT * P * 4)
    wst, _ = place("wst", [P, KT, P], F32, ub_at)
    kst, _ = place("kst", [P, KT, HALF], F32, p_hi_at, half_bytes)
    aefft, _ = place("aefft", [P, KT, BATCH * R], F32, p_lo_at, half_bytes)
    alt, _ = place("alt", [P, BATCH // BG, D], F32, p_lo_at, half_bytes + KT * BATCH * R * 4)
    tst, _ = place("tst", [P, 2, D], F32, tb_at)
    bw, _ = place("bw", [P, KT, P], F32)
    cbd, _ = place("cbd", [P, BATCH // BG, P], F32)
    bdmask, _ = place("bdmask", [P, P], F32, mgt_at)
    assert arena[0] <= nc.sbuf_usable_end, (arena[0], nc.sbuf_usable_end)
    t_dram = nc.dram_tensor("t_dram", (BATCH, 2 * R, D), F32).ap()

    bank = [nc.alloc_psum_tensor(f"bank{i}", [P, HALF], F32)[:] for i in range(8)]
    obank, sbank = bank[0:2], bank[2:4]
    zbank, midbank, mgbank, misc = bank[4], bank[5], bank[6], bank[7]

    sem = nc.alloc_semaphore
    consts_in, lora_in, shared_in, itok_in, alt_in = (sem(n) for n in ("consts_in", "lora_in", "shared_in", "itok_in", "alt_in"))
    xq_in = [sem("xq_in0"), sem("xq_in1")]
    k_in, w_in = sem("k_in"), sem("w_in")
    xbuf_in = [sem("xbuf_in0"), sem("xbuf_in1")]
    ub_in = [sem("ub_in0"), sem("ub_in1")]
    tb_in = [sem("tb_in0"), sem("tb_in1")]
    t_stored, v_stored = [sem("t_stored0"), sem("t_stored1")], sem("v_stored")
    out_stored = [sem("out_stored0"), sem("out_stored1")]
    tables, table_step, gmix_made = sem("tables"), sem("table_step"), sem("gmix_made")
    sfull, sfree = sem("sfull"), sem("sfree")
    cfull, cbd_made = sem("cfull"), sem("cbd_made")
    vfull, v_made = sem("vfull"), sem("v_made")
    t_made = sem("t_made")
    kfull, k_sum, kp_hi_made, kp_lo_made = sem("kfull"), sem("k_sum"), sem("kp_hi_made"), sem("kp_lo_made")
    w_hi_made, w_lo_made = sem("w_hi_made"), sem("w_lo_made")
    ufull, u_made = sem("ufull"), sem("u_made")
    ofull, p_hi_made, ofree = sem("ofull"), sem("p_hi_made"), sem("ofree")
    abs_made, levels_made, raised = sem("abs_made"), sem("levels_made"), sem("raised")
    valued, masked, merged, q_made = sem("valued"), sem("masked"), sem("merged"), sem("q_made")
    mid_made, gate_step, gap_made, exp_made = sem("mid_made"), sem("gate_step"), sem("gap_made"), sem("exp_made")
    mg_made, mgt_full, mgt_made = sem("mg_made"), sem("mgt_full"), sem("mgt_made")
    dfull, x1_made, x1_hi_made, x1_lo_made = sem("dfull"), sem("x1_made"), sem("x1_hi_made"), sem("x1_lo_made")
    gate_scaled = sem("gate_scaled")
    zfull, zt_made = sem("zfull"), sem("zt_made")

    PAIRS = KT // 2
    RINGS = BATCH - 2
    N_CONST = 12

    def acc(c):
        return c % 2

    def turn(c, g):
        return acc(c) if g == 0 else 2 if g % 2 else 1 - acc(c)

    def of_batch(t, u, ahead):
        return 2 * t + u + ahead, (u + ahead) % 2, t + (u + ahead) // 2

    x_v = a["xt"].rearrange("(k p) t -> p k t", p=P)
    out_v = out_t.rearrange("(k p) t -> p k t", p=P)
    w_v = a["w"].rearrange("(o p) (i c) -> i p o c", p=P, c=P)
    k_v = a["k"].rearrange("(o p) (h c) -> h p o c", p=P, c=HALF)

    with nc.allow_non_contiguous_dma(reason="rows of 1 KB and small constants"), nc.Block() as block:

        @block.gpsimd
        def _(pool):
            for c in range(2):
                pool.dma_start(xq[:, c], x_v[:, :, c * TOK:(c + 1) * TOK]).then_inc(xq_in[c], 16)
            with pool.Fori(0, RINGS // 2) as t:
                for u in range(2):
                    c, s, k = of_batch(t, u, 2)
                    pool.wait_ge(levels_made, (c - 1) * G)
                    pool.dma_start(xq[:, s], x_v[:, :, bass.ds(c * TOK, TOK)]).then_inc(xq_in[s], 16)

        @block.sync
        def _(sp):
            for dst, name in ((par, "par"), (gate_rep, "gate_rep"), (gsel, "gsel"), (bdmask, "bdmask"), (ident, "ident"), (before, "before"),
                              (ra, "ra"), (bias, "bias"), (bw, "bw"), (ber, "ber")):
                sp.dma_start(dst, a[name]).then_inc(consts_in, 16)
            sp.dma_start(tst[2 * R:3 * R, 0], a["as"]).then_inc(consts_in, 16)
            sp.dma_start(tst[2 * R:3 * R, 1], a["bst"]).then_inc(consts_in, 16)
            sp.dma_start(itok_sb, itok).then_inc(itok_in, 16)
            sp.dma_start(la, a["la"]).then_inc(lora_in, 16)
            sp.dma_start(kst, k_v[0]).then_inc(k_in, 16)
            sp.dma_start(lb, a["lb"]).then_inc(lora_in, 16)
            sp.dma_start(wst, w_v[0]).then_inc(w_in, 16)
            sp.wait_ge(itok_in, 16)
            for b in range(BATCH):
                row = sp.value_load(itok_sb[0:1, b:b + 1], min_val=0, max_val=LAB - 1)
                sp.dma_start(alt[b % BG * R:(b % BG + 1) * R, b // BG],
                             a["alt"][bass.ds(row, 1)].rearrange("o r i -> (o r) i")).then_inc(alt_in, 16)
            for g in range(NG):
                sp.wait_ge(t_made, 2 * (g + 1))
                for b in range(BATCH):
                    sp.dma_start(t_dram[b, g * RG:(g + 1) * RG], tst[b * RG:(b + 1) * RG, g % 2]).then_inc(t_stored[g % 2], 16)
            for n in range(1, STEPS):
                sp.wait_ge(w_hi_made, n)
                sp.wait_ge(w_lo_made, n)
                sp.wait_ge(ufull, min(n, KT))
                sp.dma_start(wst, w_v[n % KT]).then_inc(w_in, 16)
                if n == 1:
                    sp.wait_ge(kp_hi_made, KT)
                    sp.wait_ge(kp_lo_made, KT)
                    sp.wait_ge(vfull, 1)
                    sp.dma_start(kst, k_v[1]).then_inc(k_in, 16)
            sp.wait_ge(v_made, HALVES)
            for b in range(BATCH):
                sp.dma_start(t_dram[b, R:2 * R], tst[3 * R:4 * R, 0]).then_inc(v_stored, 16)
            for s in range(2):
                sp.wait_ge(t_stored[s], 16 * BATCH * NG // 2)
            sp.wait_ge(v_stored, 16 * BATCH)
            sp.wait_ge(ofull, STEPS)

            def adapters(b, s):
                sp.dma_start(ub[:, s, :, 0:R], uall[:, bass.ds(b, 1)].rearrange("p o k r -> p (o k) r")).then_inc(ub_in[s], 16)
                row = sp.value_load(itok_sb[0:1, bass.ds(b, 1)], min_val=0, max_val=LAB - 1)
                sp.dma_start(ub[:, s, :, R:2 * R], a["al"][bass.ds(row, 1)].rearrange("o p k r -> p (o k) r")).then_inc(ub_in[s], 16)
                sp.dma_start(tb[:, s], t_dram[bass.ds(b, 1)].rearrange("o r d -> (o r) d")).then_inc(tb_in[s], 16)

            sp.wait_ge(u_made, KT)
            for b in range(2):
                sp.dma_start(xbuf[:, b], x_v[:, :, b * TOK:(b + 1) * TOK]).then_inc(xbuf_in[b], 16)
                adapters(b, b)

            def store(b, s):
                sp.wait_ge(ofree, STEPS + (b + 1) * KT)
                sp.dma_start(out_v[:, :, bass.ds(b * TOK, TOK)], xbuf[:, s]).then_inc(out_stored[s], 16)

            with sp.Fori(0, RINGS // 2) as t:
                for u in range(2):
                    b, s, k = of_batch(t, u, 0)
                    sp.wait_ge(ofull, STEPS + (b + 1) * KT)
                    adapters(b + 2, s)
                    store(b, s)
                    sp.wait_ge(out_stored[s], 16 * (k + 1))
                    sp.dma_start(xbuf[:, s], x_v[:, :, bass.ds((b + 2) * TOK, TOK)]).then_inc(xbuf_in[s], 16)
            for b in range(RINGS, BATCH):
                store(b, b % 2)
            for s in range(2):
                sp.wait_ge(out_stored[s], 16 * BATCH // 2)

        @block.scalar
        def _(act):
            def magnitude(c, s, k):
                act.wait_ge(xq_in[s], 16 * (k + 1))
                if not (isinstance(c, int) and c == 0):
                    act.wait_ge(q_made, c)
                nc.scalar.activation(absx, xq[:, s], ACT.Abs).then_inc(abs_made, 1)

            def levels(c, s, g):
                if g >= 2:
                    act.wait_ge(raised, c * G + g - 1)
                elif not (isinstance(c, int) and c == 0):
                    act.wait_ge(raised, c * G + g - 1)
                nc.scalar.activation(level[:, g % 2], xq[:, s], ACT.Copy, scale=inv[:, g:g + 1]).then_inc(levels_made, 1)

            def raise_levels(c, s, g):
                act.wait_ge(levels_made, c * G + g + 1)
                first = isinstance(c, int) and c == 0
                if g == 2 and not first:
                    act.wait_ge(mid_made, c)
                elif g >= 3:
                    act.wait_ge(merged, c * (G - 1) + g - 2)
                elif g == 1 and not first:
                    act.wait_ge(merged, c * (G - 1))
                elif g == 0 and not first:
                    act.wait_ge(merged, c * (G - 1) - 1)
                nc.scalar.activation(val[:, turn(s, g)], level[:, g % 2], ACT.Relu, bias=shift[:, g:g + 1],
                                     scale=par[:, 1, g:g + 1]).then_inc(raised, 1)

            def quant(c, s, k, g):
                if g == 0:
                    magnitude(c, s, k)
                    levels(c, s, 0)
                if g + 1 < G:
                    levels(c, s, g + 1)
                raise_levels(c, s, g)

            def weight_hi(n):
                act.wait_ge(w_in, 16 * (n + 1))
                if n >= 2:
                    act.wait_ge(ofull, n - 1)
                nc.scalar.activation(w_hi[:, n % 2], wst, ACT.Copy).then_inc(w_hi_made, 1)

            def kp_split(h):
                for o in range(KT):
                    act.wait_ge(k_sum, h * KT + o + 1)
                    if h == 0 and o == 0:
                        act.wait_ge(sfull, KT + NG * HALVES)
                    if h == 1 and o == 0:
                        act.wait_ge(ofull, KT)
                    nc.scalar.activation(kp_hi[:, o], kst[:, o], ACT.Copy).then_inc(kp_hi_made, 1)

            def v_rows(h):
                act.wait_ge(vfull, h + 1)
                nc.scalar.activation(tst[3 * R:4 * R, 0, h * HALF:(h + 1) * HALF], misc[3 * R:4 * R], ACT.Copy,
                                     scale=LORA1).then_inc(v_made, 1)

            act.wait_ge(tables, 1)
            magnitude(0, 0, 0)
            levels(0, 0, 0)
            for o in range(KT):
                act.wait_ge(sfull, o + 1)
                nc.scalar.activation(aefft[:, o].rearrange("p (b g r) -> p b g r", b=BATCH, g=NG),
                                     sbank[o % 2][:, 0:BATCH * R].rearrange("p (g b r) -> p b g r", g=NG, b=BATCH),
                                     ACT.Copy).then_inc(sfree, 1)
            for n in range(NG * HALVES):
                g, h = divmod(n, HALVES)
                act.wait_ge(sfull, KT + n + 1)
                if g >= 2 and h == 0:
                    act.wait_ge(t_stored[g % 2], 16 * BATCH * (g // 2))
                nc.scalar.activation(tst[0:2 * R, g % 2, h * HALF:(h + 1) * HALF], sbank[n % 2][0:2 * R],
                                     ACT.Copy).then_inc(t_made, 1)
            kp_split(0)
            weight_hi(0)
            v_rows(0)
            for n in range(STEPS):
                h, i = divmod(n, KT)
                if not (n == 0):
                    quant(h, h, 0, i) if i else None
                else:
                    levels(0, 0, 1)
                    raise_levels(0, 0, 0)
                if n == KT:
                    magnitude(1, 1, 0)
                    levels(1, 1, 0)
                    levels(1, 1, 1)
                    raise_levels(1, 1, 0)
                if h == 0:
                    act.wait_ge(ufull, i + 1)
                    nc.scalar.activation(uall[:, :, i], sbank[i % 2][:, 0:BATCH * R].rearrange("p (b r) -> p b r", b=BATCH),
                                         ACT.Copy).then_inc(u_made, 1)
                if n + 1 < STEPS and n + 1 != KT:
                    weight_hi(n + 1)
                act.wait_ge(ofull, n + 1)
                nc.scalar.activation(p_hi[:, h, i], obank[n % 2], ACT.Copy).then_inc(p_hi_made, 1)
                if n == KT - 1:
                    weight_hi(KT)
                    kp_split(1)
                    v_rows(1)

            def gate_exp(c):
                act.wait_ge(gap_made, c + 1)
                nc.scalar.activation(expo, gap, ACT.Exp).then_inc(exp_made, 1)

            def gated_out(c):
                act.wait_ge(mgt_full, c + 1)
                if not (isinstance(c, int) and c == 0):
                    act.wait_ge(dfull, c * PAIRS)
                nc.scalar.activation(mgt, mgbank[0:ER, 0:TOK], ACT.Copy).then_inc(mgt_made, 1)

            def x1_part(c, s, p):
                act.wait_ge(x1_made, c * PAIRS + p + 1)
                if not (isinstance(c, int) and c < 2):
                    act.wait_ge(ofull, STEPS + (c - 1) * KT)
                nc.scalar.activation(x1_hi[:, s, 2 * p:2 * p + 2], xbuf[:, s, 2 * p:2 * p + 2], ACT.Copy).then_inc(x1_hi_made, 1)

            gate_exp(0)
            gated_out(0)
            for p in range(PAIRS):
                x1_part(0, 0, p)

            def batch(t, u, quants, follows):
                b, s, _ = of_batch(t, u, 0)
                n, ns, _ = of_batch(t, u, 1)
                c, cs, ck = of_batch(t, u, 2)
                for j in range(KT):
                    if j == 0:
                        act.wait_ge(zfull, b + 1)
                        if not (isinstance(b, int) and b == 0):
                            act.wait_ge(ofull, STEPS + b * KT)
                        nc.scalar.activation(zt, zbank[0:2 * R, 0:TOK], ACT.Copy).then_inc(zt_made, 1)
                    if quants:
                        quant(c, cs, ck, j)
                    if follows:
                        if j == 1:
                            gate_exp(n)
                        if j == 2:
                            gated_out(n)
                        if 3 <= j < 3 + PAIRS:
                            x1_part(n, ns, j - 3)

            with act.Fori(0, RINGS // 2) as t:
                for u in range(2):
                    batch(t, u, True, True)
            batch(RINGS // 2, 0, False, True)
            batch(RINGS // 2, 1, False, False)

        @block.vector
        def _(dve):
            def value(c, s, g):
                dve.wait_ge(raised, c * G + g + 1)
                v = val[:, turn(s, g)]
                nc.vector.tensor_scalar(v, v, width[:, g:g + 1], unshift[:, g:g + 1], ALU.min, ALU.add).then_inc(valued, 1)

            def mask(c, g):
                if g == 1:
                    dve.wait_ge(abs_made, c + 1)
                nc.vector.tensor_scalar(inside[:, g % 2], absx, thr[:, g - 1:g], None, ALU.is_le).then_inc(masked, 1)

            def before_merge(c, g):
                dve.wait_ge(valued, c * G + g + 1)
                dve.wait_ge(masked, c * (G - 1) + g)
                if g >= 2:
                    dve.wait_ge(merged, c * (G - 1) + g - 1)

            def merge(s, g):
                nc.vector.copy_predicated(val[:, acc(s)], inside[:, g % 2], val[:, turn(s, g)]).then_inc(merged, 1)

            def finish(c, s):
                dve.wait_ge(merged, (c + 1) * (G - 1))
                nc.vector.scalar_tensor_tensor(val[:, acc(s)], absx, thr[:, G - 1:G], val[:, acc(s)],
                                               ALU.is_gt, ALU.mult).then_inc(q_made, 1)

            def quant(c, s, g):
                value(c, s, g)
                if g:
                    before_merge(c, g)
                if g + 1 < G:
                    mask(c, g + 1)
                else:
                    nc.vector.memset(idle, 0.0)
                if g:
                    merge(s, g)
                if g + 1 == G:
                    finish(c, s)

            def weight_lo(n):
                dve.wait_ge(w_hi_made, n + 1)
                if n >= 2:
                    dve.wait_ge(ofull, n - 1)
                nc.vector.tensor_tensor(w_lo[:, n % 2], wst, w_hi[:, n % 2].bitcast(F32), ALU.subtract).then_inc(w_lo_made, 1)

            def k_add(h):
                for o in range(KT):
                    dve.wait_ge(kfull, h * KT + o + 1)
                    nc.vector.tensor_tensor(kst[:, o], sbank[o % 2], kst[:, o], ALU.add).then_inc(k_sum, 1)

            def kp_lo_part(h):
                for o in range(KT):
                    dve.wait_ge(kp_hi_made, h * KT + o + 1)
                    nc.vector.tensor_tensor(kp_lo[:, o], kst[:, o], kp_hi[:, o].bitcast(F32), ALU.subtract).then_inc(kp_lo_made, 1)

            dve.wait_ge(consts_in, 16 * N_CONST)
            nc.vector.tensor_tensor(gmix, gate_rep.unsqueeze(2).to_broadcast([P, BATCH, RG]),
                                    gsel.unsqueeze(1).to_broadcast([P, BATCH, RG]), ALU.mult).then_inc(gmix_made, 1)
            nc.vector.max(thr, par[:, 0])
            nc.vector.reciprocal(inv, par[:, 1])
            nc.vector.tensor_scalar(width, par[:, 1], LEVELS, None, ALU.mult)
            nc.vector.tensor_tensor(shift, par[:, 1], par[:, 2], ALU.mult).then_inc(table_step, 1)
            dve.wait_ge(table_step, 1)
            nc.vector.tensor_scalar(unshift, shift, -1.0, None, ALU.mult).then_inc(tables, 1)
            dve.wait_ge(cfull, 1)
            for q in range(BATCH // BG):
                last = nc.vector.scalar_tensor_tensor(cbd[:, q], misc[:, q * P:(q + 1) * P], LORA1, bdmask, ALU.mult, ALU.mult)
            last.then_inc(cbd_made, 1)
            dve.wait_ge(k_in, 16)
            k_add(0)
            kp_lo_part(0)
            weight_lo(0)
            dve.wait_ge(tables, 1)
            for n in range(STEPS):
                h, i = divmod(n, KT)
                quant(h, h, i)
                if n + 1 < STEPS and n + 1 != KT:
                    weight_lo(n + 1)
                if n == KT - 1:
                    dve.wait_ge(k_in, 32)
                    k_add(1)
                dve.wait_ge(p_hi_made, n + 1)
                nc.vector.tensor_tensor(p_lo[:, h, i], obank[n % 2], p_hi[:, h, i].bitcast(F32), ALU.subtract).then_inc(ofree, 1)
                if n == KT - 1:
                    weight_lo(KT)
                    kp_lo_part(1)

            GATE_STEPS = 10
            def gate(c):
                done = [0]

                def then(ins):
                    done[0] += 1
                    ins.then_inc(gate_step, 1)
                    dve.wait_ge(gate_step, c * GATE_STEPS + done[0])

                mid = midbank[:, 0:TT * RT].rearrange("p (t m) -> p t m", t=TT)
                dve.wait_ge(mid_made, c + 1)
                then(nc.vector.tensor_copy(lg, mid[:, :, ER:RT]))
                then(nc.vector.reduce_max(best, lg, AX))
                nc.vector.tensor_tensor(gap, lg, best.unsqueeze(2).to_broadcast([P, TT, E]), ALU.subtract).then_inc(gap_made, 1)
                mine = lg.unsqueeze(3).to_broadcast([P, TT, E, E])
                other = lg.unsqueeze(2).to_broadcast([P, TT, E, E])
                then(nc.vector.tensor_tensor(ties, other, mine, ALU.is_equal))
                then(nc.vector.tensor_tensor(ties, ties, before, ALU.mult))
                then(nc.vector.tensor_tensor(beats, other, mine, ALU.is_gt))
                then(nc.vector.tensor_tensor(beats, beats, ties, ALU.add))
                then(nc.vector.reduce_sum(rank, beats, AX))
                dve.wait_ge(exp_made, c + 1)
                then(nc.vector.scalar_tensor_tensor(gates, rank, TOP_K, expo, ALU.is_lt, ALU.mult))
                then(nc.vector.reduce_sum(total, gates, AX))
                then(nc.vector.reciprocal(total, total))
                nc.vector.scalar_tensor_tensor(gates, gates, LORA0, total.unsqueeze(2).to_broadcast([P, TT, E]),
                                               ALU.mult, ALU.mult).then_inc(gate_scaled, 1)
                dve.wait_ge(gate_scaled, c + 1)
                nc.vector.tensor_tensor(mg.rearrange("p t (e r) -> p t e r", e=E), mid[:, :, 0:ER].rearrange("p t (e r) -> p t e r", e=E),
                                        gates.unsqueeze(3).to_broadcast([P, TT, E, R0]), ALU.mult).then_inc(mg_made, 1)

            def x1_sum(c, s, k, p):
                dve.wait_ge(dfull, c * PAIRS + p + 1)
                if p == 0:
                    dve.wait_ge(xbuf_in[s], 16 * (k + 1))
                pair = xbuf[:, s, 2 * p:2 * p + 2].rearrange("p k t -> p (k t)")
                nc.vector.tensor_tensor(pair, sbank[p % 2], pair, ALU.add).then_inc(x1_made, 1)

            def x1_part(c, s, p):
                dve.wait_ge(x1_hi_made, c * PAIRS + p + 1)
                nc.vector.tensor_tensor(x1_lo[:, s, 2 * p:2 * p + 2], xbuf[:, s, 2 * p:2 * p + 2],
                                        x1_hi[:, s, 2 * p:2 * p + 2].bitcast(F32), ALU.subtract).then_inc(x1_lo_made, 1)

            gate(0)
            for p in range(PAIRS):
                x1_sum(0, 0, 0, p)
                x1_part(0, 0, p)

            def batch(t, u, quants, follows):
                b, s, _ = of_batch(t, u, 0)
                n, ns, nk = of_batch(t, u, 1)
                c, cs, _ = of_batch(t, u, 2)
                for j in range(KT):
                    if quants:
                        quant(c, cs, j)
                    if follows:
                        if j == 0:
                            gate(n)
                        if 4 <= j < 4 + PAIRS:
                            x1_part(n, ns, j - 4)
                        if 3 <= j < 3 + PAIRS:
                            x1_sum(n, ns, nk, j - 3)
                    dve.wait_ge(ofull, STEPS + b * KT + j + 1)
                    nc.vector.scalar_tensor_tensor(xbuf[:, s, j], obank[j % 2][:, 0:TOK], bias[:, j:j + 1], xbuf[:, s, j],
                                                   ALU.add, ALU.add).then_inc(ofree, 1)

            with dve.Fori(0, RINGS // 2) as t:
                for u in range(2):
                    batch(t, u, True, True)
            batch(RINGS // 2, 0, False, True)
            batch(RINGS // 2, 1, False, False)

        @block.tensor
        def _(pe):
            mm = nc.tensor.matmul
            gm = gmix.rearrange("p b r -> p (b r)")
            pe.wait_ge(gmix_made, 1)
            pe.wait_ge(lora_in, 32)
            for o in range(KT):
                if o >= 2:
                    pe.wait_ge(sfree, o - 1)
                for g in range(NG):
                    last = mm(sbank[o % 2][:, g * BATCH * RG:(g + 1) * BATCH * RG], la[:, g, o * P:(o + 1) * P], gm, start=True, stop=True)
                last.then_inc(sfull, 1)
            for n in range(NG * HALVES):
                g, h = divmod(n, HALVES)
                if n < 2:
                    pe.wait_ge(sfree, KT - 1 + n)
                else:
                    pe.wait_ge(t_made, n - 1)
                mm(sbank[n % 2][0:2 * R], gm, lb[:, g, h * HALF:(h + 1) * HALF], start=True, stop=True).then_inc(sfull, 1)
            pe.wait_ge(sfree, KT)
            for o in range(KT):
                last = mm(misc[:, 0:BATCH * R], bw[:, o], aefft[:, o], start=o == 0, stop=o == KT - 1)
            last.then_inc(cfull, 1)

            def k_update(h):
                for o in range(KT):
                    if o >= 2:
                        pe.wait_ge(k_sum, h * KT + o - 1)
                    elif h == 0:
                        pe.wait_ge(t_made, NG * HALVES - 1 + o)
                    else:
                        pe.wait_ge(u_made, KT - 1 + o)
                    mm(sbank[o % 2], tst[2 * R:3 * R, 0, o * P:(o + 1) * P], tst[2 * R:3 * R, 1, h * HALF:(h + 1) * HALF],
                       start=True, stop=True).then_inc(kfull, 1)

            def v_product(h):
                pe.wait_ge(k_sum, (h + 1) * KT)
                if h == 0:
                    pe.wait_ge(cbd_made, 1)
                else:
                    pe.wait_ge(v_made, 1)
                for o in range(KT):
                    last = mm(misc, bw[:, o], kst[:, o], start=o == 0, stop=o == KT - 1)
                last.then_inc(vfull, 1)

            k_update(0)
            v_product(0)

            def mid(c, s):
                pe.wait_ge(q_made, c + 1)
                if not (isinstance(c, int) and c == 0):
                    pe.wait_ge(mg_made, c)
                for t in range(TT):
                    for k in range(KT):
                        last = mm(midbank[:, t * RT:(t + 1) * RT], val[:, acc(s), k, t * P:(t + 1) * P], ra[:, k],
                                  start=k == 0, stop=k == KT - 1)
                last.then_inc(mid_made, 1)

            def gated_turn(c):
                pe.wait_ge(mg_made, c + 1)
                if not (isinstance(c, int) and c == 0):
                    pe.wait_ge(mgt_made, c)
                for t in range(TT):
                    last = mm(mgbank[0:ER, t * P:(t + 1) * P], mg[:, t], ident, start=True, stop=True)
                last.then_inc(mgt_full, 1)

            def layer0(c, p):
                pe.wait_ge(mgt_made, c + 1)
                if not (isinstance(c, int) and c == 0 and p < 2):
                    pe.wait_ge(x1_made, c * PAIRS + p - 1)
                for k in (2 * p, 2 * p + 1):
                    last = mm(sbank[p % 2][:, k % 2 * TOK:(k % 2 + 1) * TOK], ber[:, k * P:(k + 1) * P], mgt, start=True, stop=True)
                last.then_inc(dfull, 1)

            pe.wait_ge(alt_in, 16 * BATCH)
            for n in range(STEPS):
                h, i = divmod(n, KT)
                if h == 0:
                    pe.wait_ge(w_in, 16 * (n + 1))
                    if i < 2:
                        pe.wait_ge(k_sum, KT - 1 + i)
                    else:
                        pe.wait_ge(u_made, i - 1)
                    for o in range(KT):
                        mm(sbank[i % 2][:, 0:BATCH * R], wst[:, o], aefft[:, o], start=o == 0, stop=False)
                    for q in range(BATCH // BG):
                        last = mm(sbank[i % 2][:, q * P:(q + 1) * P], alt[:, q, i * P:(i + 1) * P], cbd[:, q],
                                  start=False, stop=q == BATCH // BG - 1)
                    last.then_inc(ufull, 1)
                if n == KT - 1:
                    k_update(1)
                pe.wait_ge(w_lo_made, n + 1)
                if n >= 2:
                    pe.wait_ge(ofree, n - 1)
                for o in range(KT):
                    if i == 0:
                        pe.wait_ge(kp_lo_made, h * KT + o + 1)
                    mm(obank[n % 2], w_hi[:, n % 2, o], kp_hi[:, o], start=o == 0, stop=False)
                    mm(obank[n % 2], w_hi[:, n % 2, o], kp_lo[:, o], start=False, stop=False)
                    last = mm(obank[n % 2], w_lo[:, n % 2, o], kp_hi[:, o], start=False, stop=o == KT - 1)
                last.then_inc(ofull, 1)
                if n == KT - 1:
                    v_product(1)
                if n == KT:
                    mid(0, 0)
            gated_turn(0)
            for p in range(PAIRS):
                layer0(0, p)

            def low_rank(b, s, j):
                mm(obank[j % 2][:, 0:TOK], tb[:, s, j * P:(j + 1) * P], zt, start=False, stop=True).then_inc(ofull, 1)

            def batch(t, u, follows):
                b, s, sk = of_batch(t, u, 0)
                n, ns, _ = of_batch(t, u, 1)
                pe.wait_ge(x1_made, (b + 1) * PAIRS)
                pe.wait_ge(ub_in[s], 32 * (sk + 1))
                for k in range(KT):
                    last = mm(zbank[0:2 * R, 0:TOK], ub[:, s, k], xbuf[:, s, k], start=k == 0, stop=k == KT - 1)
                last.then_inc(zfull, 1)
                if follows:
                    mid(n, ns)
                pe.wait_ge(x1_lo_made, (b + 1) * PAIRS)
                for j in range(KT):
                    h, at = j // (KT // 2), j % (KT // 2) * P
                    pe.wait_ge(ofree, STEPS + b * KT + j - 1)
                    for k in range(KT):
                        mm(obank[j % 2][:, 0:TOK], p_hi[:, h, k, at:at + P], x1_hi[:, s, k], start=k == 0, stop=False)
                        mm(obank[j % 2][:, 0:TOK], p_hi[:, h, k, at:at + P], x1_lo[:, s, k], start=False, stop=False)
                        mm(obank[j % 2][:, 0:TOK], p_lo[:, h, k, at:at + P], x1_hi[:, s, k], start=False, stop=False)
                    if j == 0:
                        pe.wait_ge(zt_made, b + 1)
                        pe.wait_ge(tb_in[s], 16 * (sk + 1))
                    low_rank(b, s, j)
                    if follows:
                        if j == 1:
                            gated_turn(n)
                        if 2 <= j < 2 + PAIRS:
                            layer0(n, j - 2)

            with pe.Fori(0, RINGS // 2) as t:
                for u in range(2):
                    batch(t, u, True)
            batch(RINGS // 2, 0, True)
            batch(RINGS // 2, 1, False)


def kernel(**inputs):
    import concourse.bacc as bacc
    from concourse.bass_utils import run_bass_kernel_spmd

    v = {k: np.asarray(x) for k, x in inputs.items()}
    c = np.ascontiguousarray
    i4, i16 = np.arange(E), np.arange(P)
    before = np.broadcast_to((i4[None, :] < i4[:, None]).astype(np.float32), (P, TT, E, E))
    arrays = {
        "xt": c(v["x"].reshape(BATCH * TOK, D).T),
        "par": c(np.broadcast_to(np.stack([v["condB_thresholds"], v["condB_deltas"], v["condB_zeropoints"]]), (P, 3, G))),
        "ra": c(np.concatenate([v["L0_ffn_A"].reshape(ER, D), v["L0_ffn_router_w"]]).reshape(RT, KT, P).transpose(2, 1, 0)),
        "ber": c(v["L0_ffn_B"].transpose(0, 2, 1).reshape(ER, D)),
        "w": c(v["L1_cond_W"]),
        "k": c(v["L1_ffn_kernel"]),
        "as": c(v["L1_ffn_lora_A_shared"]),
        "bst": c(v["L1_ffn_lora_B_shared"].T),
        "la": c(v["L1_ffn_lora_A"].transpose(1, 0, 2).reshape(NG, P, D).transpose(1, 0, 2)),
        "lb": c(v["L1_ffn_lora_B"].transpose(2, 0, 1).reshape(NG, P, D).transpose(1, 0, 2)),
        "gate_rep": c(np.tile(v["L1_ffn_gate"].T, (RG, 1))),
        "bw": c(np.tile(v["L1_cond_lora_B_w"].reshape(KT, P, R).transpose(1, 0, 2), (1, 1, BG))),
        "al": c(v["L1_cond_lora_A"].reshape(LAB, KT, P, R).transpose(0, 2, 1, 3)),
        "alt": c(v["L1_cond_lora_A"].transpose(0, 2, 1)),
        "bias": c(v["L1_ffn_bias"].reshape(KT, P).T),
        "gsel": (i16[:, None] // NL == np.arange(RG)[None, :]).astype(np.float32),
        "bdmask": (i16[:, None] // R == i16[None, :] // R).astype(np.float32),
        "ident": np.eye(P, dtype=np.float32),
        "before": c(before),
        "itok": c(v["itok_B_0_2"].reshape(1, BATCH)),
    }
    nc = bacc.Bacc("TRN2", target_bir_lowering=False, num_devices=1)
    aps = {k: nc.dram_tensor(f"{k}_in", x.shape, mybir.dt.from_np(x.dtype), kind="ExternalInput").ap() for k, x in arrays.items()}
    out_t = nc.dram_tensor("out_t", (D, BATCH * TOK), F32, kind="ExternalOutput").ap()
    itok = aps.pop("itok")
    build(nc, aps, out_t, itok)
    r = run_bass_kernel_spmd(nc, [{f"{k}_in": x for k, x in arrays.items()}], core_ids=[0])
    return c(r.results[0]["out_t"].T).reshape(BATCH, TOK, D)
```

```python
import numpy as np
import concourse.bass as bass
from concourse import mybir

F32 = mybir.dt.float32
F32R = mybir.dt.float32r
I16 = mybir.dt.int16
I32 = mybir.dt.int32
U8 = mybir.dt.uint8
ALU = mybir.AluOpType
ACT = mybir.ActivationFunctionType
AX = mybir.AxisListType.X

P = 128
BATCH = 8
TOK = 256
TT = TOK // P
D = 1024
KT = D // P
G = 8
E, R0 = 4, 16
ER = E * R0
RT = ER + E
R = 32
NL = 16
RG = P // NL
NG = R // RG
LAB = 5
HALF = D // 2
HALVES = 2
STEPS = HALVES * KT
BG = P // R
LEVELS = 63.0
TOP_K = 2.0
LORA0 = 4.0
LORA1 = 0.5


def build(nc, a, out_t, itok):
    arena = [(nc.sbuf_base + 31) // 32 * 32]

    def place(name, shape, dt, at=None, after=0):
        size = int(np.prod(shape[1:])) * mybir.dt.size(dt)
        size = (size + 31) // 32 * 32
        if at is None:
            at = arena[0]
            arena[0] += size
        t = nc.alloc_sbuf_tensor_at(name, shape, dt, offset=at + after)
        return t[:], at

    p_hi, _ = place("p_hi", [P, HALVES, KT, HALF], F32R)
    p_lo, p_lo_at = place("p_lo", [P, HALVES, KT, HALF], F32R)
    p_hi_at = p_lo_at - HALVES * KT * HALF * 4
    half_bytes = KT * HALF * 4
    val, _ = place("val", [P, 3, KT, TOK], F32)
    absx, _ = place("absx", [P, KT, TOK], F32)
    level, _ = place("level", [P, 2, KT, TOK], I16)
    inside, _ = place("inside", [P, 2, KT, TOK], U8)
    xq, _ = place("xq", [P, 2, KT, TOK], F32)
    xbuf, xbuf_at = place("xbuf", [P, 2, KT, TOK], F32)
    x1_hi, x1_at = place("x1_hi", [P, 2, KT, TOK], F32R)
    x1_lo, x1_lo_at = place("x1_lo", [P, 2, KT, TOK], F32R)
    ub, ub_at = place("ub", [P, 2, KT, 2 * R], F32)
    tb, tb_at = place("tb", [2 * R, 2, D], F32)
    uall, _ = place("uall", [P, BATCH, KT, R], F32)
    ra, _ = place("ra", [P, KT, RT], F32)
    ber, _ = place("ber", [ER, D], F32)
    mg, _ = place("mg", [P, TT, ER], F32)
    mgt, mgt_at = place("mgt", [ER, TOK], F32)
    zt, zt_at = place("zt", [2 * R, TOK], F32)
    ident, _ = place("ident", [P, P], F32R)
    bias, _ = place("bias", [P, KT], F32)
    par, _ = place("par", [P, 3, G], F32)
    thr, _ = place("thr", [P, G], F32)
    inv, _ = place("inv", [P, G], F32)
    shift, _ = place("shift", [P, G], F32)
    unshift, _ = place("unshift", [P, G], F32)
    width, _ = place("width", [P, G], F32)
    before, _ = place("before", [P, TT, E, E], F32)
    lg, _ = place("lg", [P, TT, E], F32)
    beats, _ = place("beats", [P, TT, E, E], F32)
    ties, _ = place("ties", [P, TT, E, E], F32)
    rank, _ = place("rank", [P, TT, E], F32)
    best, _ = place("best", [P, TT], F32)
    gap, _ = place("gap", [P, TT, E], F32)
    expo, _ = place("expo", [P, TT, E], F32)
    gates, _ = place("gates", [P, TT, E], F32)
    total, _ = place("total", [P, TT], F32)
    idle, _ = place("idle", [P, 1], F32)
    itok_sb, _ = place("itok_sb", [1, BATCH], I32)
    gate_rep, _ = place("gate_rep", [P, BATCH], F32)
    gsel, _ = place("gsel", [P, RG], F32)
    gmix, _ = place("gmix", [P, BATCH, RG], F32)
    la, _ = place("la", [P, NG, D], F32, p_hi_at)
    lb, _ = place("lb", [P, NG, D], F32, p_lo_at)
    kst, _ = place("kst", [P, KT, HALF], F32, p_hi_at, half_bytes)
    aefft, _ = place("aefft", [P, KT, BATCH * R], F32, p_lo_at, half_bytes)
    alt, _ = place("alt", [P, BATCH // BG, D], F32, p_lo_at, half_bytes + KT * BATCH * R * 4)
    kp_hi, _ = place("kp_hi", [P, KT, HALF], F32R, x1_at)
    kp_lo, _ = place("kp_lo", [P, KT, HALF], F32R, x1_lo_at)
    w_bytes = KT * P * 4
    w_hi = [place(f"w_hi{i}", [P, KT, P], F32R, xbuf_at, 2 * i * w_bytes)[0] for i in range(2)]
    w_lo = [place(f"w_lo{i}", [P, KT, P], F32R, xbuf_at, (2 * i + 1) * w_bytes)[0] for i in range(2)]
    wst, _ = place("wst", [P, KT, P], F32, ub_at)
    ident_raw, _ = place("ident_raw", [P, P], F32, zt_at)
    tst, _ = place("tst", [P, 2, D], F32, tb_at)
    bw, _ = place("bw", [P, KT, P], F32)
    cbd, _ = place("cbd", [P, BATCH // BG, P], F32)
    bdmask, _ = place("bdmask", [P, P], F32, mgt_at)
    assert arena[0] <= nc.sbuf_usable_end, (arena[0], nc.sbuf_usable_end)
    t_dram = nc.dram_tensor("t_dram", (BATCH, 2 * R, D), F32).ap()

    bank = [nc.alloc_psum_tensor(f"bank{i}", [P, HALF], F32)[:] for i in range(8)]
    obank, sbank = bank[0:4], bank[4:6]
    zbank, midbank = bank[6], bank[7]
    misc = zbank
    mgbank = midbank[:, HALF // 2:HALF]

    sem = nc.alloc_semaphore
    consts_in, lora_in, lb_in, shared_in, itok_in, alt_in, ra_in = (
        sem(n) for n in ("consts_in", "lora_in", "lb_in", "shared_in", "itok_in", "alt_in", "ra_in"))
    xq_in = [sem("xq_in0"), sem("xq_in1")]
    k_in, w_in = sem("k_in"), sem("w_in")
    xbuf_in = [sem("xbuf_in0"), sem("xbuf_in1")]
    ub_in = [sem("ub_in0"), sem("ub_in1")]
    tb_in = [sem("tb_in0"), sem("tb_in1")]
    t_stored, v_stored = [sem("t_stored0"), sem("t_stored1")], sem("v_stored")
    out_stored = [sem("out_stored0"), sem("out_stored1")]
    ident_made = sem("ident_made")
    tables, table_step, gmix_made = sem("tables"), sem("table_step"), sem("gmix_made")
    sfull, sfree = sem("sfull"), sem("sfree")
    cfull, cbd_made = sem("cfull"), sem("cbd_made")
    vfull, v_made = sem("vfull"), sem("v_made")
    t_made = sem("t_made")
    kfull, k_sum, kp_hi_made, kp_lo_made = sem("kfull"), sem("k_sum"), sem("kp_hi_made"), sem("kp_lo_made")
    w_hi_made, w_lo_made = sem("w_hi_made"), sem("w_lo_made")
    ufull, u_made = sem("ufull"), sem("u_made")
    ofull, p_hi_made, ofree = sem("ofull"), sem("p_hi_made"), sem("ofree")
    abs_made, levels_made, raised = sem("abs_made"), sem("levels_made"), sem("raised")
    valued, masked, merged, q_made = sem("valued"), sem("masked"), sem("merged"), sem("q_made")
    mid_made, gate_step, gap_made, exp_made = sem("mid_made"), sem("gate_step"), sem("gap_made"), sem("exp_made")
    mg_made, mgt_full, mgt_made = sem("mg_made"), sem("mgt_full"), sem("mgt_made")
    dfull, x1_made, x1_hi_made, x1_lo_made = sem("dfull"), sem("x1_made"), sem("x1_hi_made"), sem("x1_lo_made")
    gate_scaled = sem("gate_scaled")
    zfull, zt_made = sem("zfull"), sem("zt_made")

    PAIRS = KT // 2
    RINGS = BATCH - 2
    RING = len(obank)
    N_CONST = 7

    AHEAD = [(0, 0), (0, 1)]
    TAKEN = [1, 2, 1, 2, 1, 1, 1, 1, 1, 0, 1, 0, 1, 1, 0, 0]
    MID0 = 5
    order = [(c, g) for c in range(2) for g in range(G)][len(AHEAD):]
    GROUPS = [[order.pop(0) for _ in range(m)] for m in TAKEN]
    assert not order

    def acc(c):
        return c % 2

    def turn(c, g):
        return acc(c) if g == 0 else 2 if g % 2 else 1 - acc(c)

    def of_batch(t, u, ahead):
        return 2 * t + u + ahead, (u + ahead) % 2, t + (u + ahead) // 2

    x_v = a["xt"].rearrange("(k p) t -> p k t", p=P)
    out_v = out_t.rearrange("(k p) t -> p k t", p=P)
    w_v = a["w"].rearrange("(o p) (i c) -> i p o c", p=P, c=P)
    k_v = a["k"].rearrange("(o p) (h c) -> h p o c", p=P, c=HALF)

    with nc.allow_non_contiguous_dma(reason="rows of 1 KB and small constants"), nc.Block() as block:

        @block.gpsimd
        def _(pool):
            for c in range(2):
                pool.dma_start(xq[:, c], x_v[:, :, c * TOK:(c + 1) * TOK]).then_inc(xq_in[c], 16)
            with pool.Fori(0, RINGS // 2) as t:
                for u in range(2):
                    c, s, k = of_batch(t, u, 2)
                    pool.wait_ge(levels_made, (c - 1) * G)
                    pool.dma_start(xq[:, s], x_v[:, :, bass.ds(c * TOK, TOK)]).then_inc(xq_in[s], 16)

        @block.sync
        def _(sp):
            for dst, name in ((par, "par"), (gate_rep, "gate_rep"), (gsel, "gsel"), (bdmask, "bdmask"), (ident_raw, "ident"),
                              (before, "before"), (bias, "bias")):
                sp.dma_start(dst, a[name]).then_inc(consts_in, 16)
            sp.dma_start(la, a["la"]).then_inc(lora_in, 16)
            sp.dma_start(tst[2 * R:3 * R, 0], a["as"]).then_inc(shared_in, 16)
            sp.dma_start(tst[2 * R:3 * R, 1], a["bst"]).then_inc(shared_in, 16)
            sp.dma_start(kst, k_v[0]).then_inc(k_in, 16)
            sp.dma_start(bw, a["bw"]).then_inc(shared_in, 16)
            sp.dma_start(itok_sb, itok).then_inc(itok_in, 16)
            sp.dma_start(wst, w_v[0]).then_inc(w_in, 16)
            sp.dma_start(lb, a["lb"]).then_inc(lb_in, 16)
            sp.dma_start(ra, a["ra"]).then_inc(ra_in, 16)
            sp.dma_start(ber, a["ber"]).then_inc(ra_in, 16)
            sp.wait_ge(itok_in, 16)
            for b in range(BATCH):
                row = sp.value_load(itok_sb[0:1, b:b + 1], min_val=0, max_val=LAB - 1)
                sp.dma_start(alt[b % BG * R:(b % BG + 1) * R, b // BG],
                             a["alt"][bass.ds(row, 1)].rearrange("o r i -> (o r) i")).then_inc(alt_in, 16)
            for g in range(NG):
                sp.wait_ge(t_made, 2 * (g + 1))
                for b in range(BATCH):
                    sp.dma_start(t_dram[b, g * RG:(g + 1) * RG], tst[b * RG:(b + 1) * RG, g % 2]).then_inc(t_stored[g % 2], 16)
            def adapters(b, s):
                sp.dma_start(ub[:, s, :, 0:R], uall[:, bass.ds(b, 1)].rearrange("p o k r -> p (o k) r")).then_inc(ub_in[s], 16)
                row = sp.value_load(itok_sb[0:1, bass.ds(b, 1)], min_val=0, max_val=LAB - 1)
                sp.dma_start(ub[:, s, :, R:2 * R], a["al"][bass.ds(row, 1)].rearrange("o p k r -> p (o k) r")).then_inc(ub_in[s], 16)

            def rows(b, s):
                sp.dma_start(tb[:, s], t_dram[bass.ds(b, 1)].rearrange("o r d -> (o r) d")).then_inc(tb_in[s], 16)

            for n in range(1, STEPS):
                sp.wait_ge(w_hi_made, n)
                sp.wait_ge(w_lo_made, n)
                sp.wait_ge(ufull, min(n, KT))
                sp.dma_start(wst, w_v[n % KT]).then_inc(w_in, 16)
                if n == 1:
                    sp.wait_ge(kp_hi_made, KT)
                    sp.wait_ge(kp_lo_made, KT)
                    sp.wait_ge(vfull, 1)
                    sp.dma_start(kst, k_v[1]).then_inc(k_in, 16)
                if n == KT + 1:
                    sp.wait_ge(v_made, HALVES)
                    for b in range(BATCH):
                        sp.dma_start(t_dram[b, R:2 * R], tst[3 * R:4 * R, 0]).then_inc(v_stored, 16)
                if n == KT + 2:
                    for s in range(2):
                        sp.wait_ge(t_stored[s], 16 * BATCH * NG // 2)
                    sp.wait_ge(v_stored, 16 * BATCH)
                    for b in range(2):
                        rows(b, b)
            sp.wait_ge(w_hi_made, STEPS)
            sp.wait_ge(w_lo_made, STEPS)
            sp.wait_ge(u_made, KT)
            for b in range(2):
                adapters(b, b)
            for b in range(2):
                sp.wait_ge(ofull, STEPS - 1 + b)
                sp.dma_start(xbuf[:, b], x_v[:, :, b * TOK:(b + 1) * TOK]).then_inc(xbuf_in[b], 16)

            def store(b, s):
                sp.wait_ge(ofree, STEPS + (b + 1) * KT)
                sp.dma_start(out_v[:, :, bass.ds(b * TOK, TOK)], xbuf[:, s]).then_inc(out_stored[s], 16)

            with sp.Fori(0, RINGS // 2) as t:
                for u in range(2):
                    b, s, k = of_batch(t, u, 0)
                    sp.wait_ge(ofull, STEPS + (b + 1) * KT)
                    adapters(b + 2, s)
                    rows(b + 2, s)
                    store(b, s)
                    sp.wait_ge(out_stored[s], 16 * (k + 1))
                    sp.dma_start(xbuf[:, s], x_v[:, :, bass.ds((b + 2) * TOK, TOK)]).then_inc(xbuf_in[s], 16)
            for b in range(RINGS, BATCH):
                store(b, b % 2)
            for s in range(2):
                sp.wait_ge(out_stored[s], 16 * BATCH // 2)

        @block.scalar
        def _(act):
            def magnitude(c, s, k):
                act.wait_ge(xq_in[s], 16 * (k + 1))
                if not (isinstance(c, int) and c == 0):
                    act.wait_ge(q_made, c)
                nc.scalar.activation(absx, xq[:, s], ACT.Abs).then_inc(abs_made, 1)

            def levels(c, s, g):
                if g >= 2:
                    act.wait_ge(raised, c * G + g - 1)
                elif not (isinstance(c, int) and c == 0):
                    act.wait_ge(raised, c * G + g - 1)
                nc.scalar.activation(level[:, g % 2], xq[:, s], ACT.Copy, scale=inv[:, g:g + 1]).then_inc(levels_made, 1)

            def raise_levels(c, s, g):
                act.wait_ge(levels_made, c * G + g + 1)
                first = isinstance(c, int) and c == 0
                if g == 2 and not first:
                    act.wait_ge(mid_made, c)
                elif g >= 3:
                    act.wait_ge(merged, c * (G - 1) + g - 2)
                elif g == 1 and not first:
                    act.wait_ge(merged, c * (G - 1))
                elif g == 0 and not first:
                    act.wait_ge(merged, c * (G - 1) - 1)
                nc.scalar.activation(val[:, turn(s, g)], level[:, g % 2], ACT.Relu, bias=shift[:, g:g + 1],
                                     scale=par[:, 1, g:g + 1]).then_inc(raised, 1)

            def quant(c, s, k, g):
                if g + 1 < G:
                    levels(c, s, g + 1)
                raise_levels(c, s, g)

            def weight_hi(n):
                act.wait_ge(w_in, 16 * (n + 1))
                if n >= 2:
                    act.wait_ge(ofull, n - 1)
                nc.scalar.activation(w_hi[n % 2], wst, ACT.Copy).then_inc(w_hi_made, 1)

            def kp_split(h):
                for o in range(KT):
                    act.wait_ge(k_sum, h * KT + o + 1)
                    if h == 1 and o == 0:
                        act.wait_ge(ofull, KT)
                    nc.scalar.activation(kp_hi[:, o], kst[:, o], ACT.Copy).then_inc(kp_hi_made, 1)

            def v_rows(h):
                act.wait_ge(vfull, h + 1)
                nc.scalar.activation(tst[3 * R:4 * R, 0, h * HALF:(h + 1) * HALF], misc[3 * R:4 * R], ACT.Copy,
                                     scale=LORA1).then_inc(v_made, 1)

            def gate_exp(c):
                act.wait_ge(gap_made, c + 1)
                nc.scalar.activation(expo, gap, ACT.Exp).then_inc(exp_made, 1)

            def gated_out(c):
                act.wait_ge(mgt_full, c + 1)
                if not (isinstance(c, int) and c == 0):
                    act.wait_ge(dfull, c * PAIRS)
                nc.scalar.activation(mgt, mgbank[0:ER, 0:TOK], ACT.Copy).then_inc(mgt_made, 1)

            def prologue_quant(c, g):
                if g == 0:
                    act.wait_ge(xq_in[c], 16)
                    levels(c, c, 0)
                quant(c, c, 0, g)
                if g == 0 and c:
                    magnitude(c, c, 0)

            act.wait_ge(tables, 1)
            nc.scalar.activation(ident, ident_raw, ACT.Copy).then_inc(ident_made, 1)
            magnitude(0, 0, 0)
            for o in range(KT):
                act.wait_ge(sfull, o + 1)
                nc.scalar.activation(aefft[:, o].rearrange("p (b g r) -> p b g r", b=BATCH, g=NG),
                                     sbank[o % 2][:, 0:BATCH * R].rearrange("p (g b r) -> p b g r", g=NG, b=BATCH),
                                     ACT.Copy).then_inc(sfree, 1)
                if o == KT // 2:
                    prologue_quant(*AHEAD[0])
            prologue_quant(*AHEAD[1])
            kp_split(0)
            weight_hi(0)
            for n in range(NG * HALVES):
                g, h = divmod(n, HALVES)
                act.wait_ge(sfull, KT + n + 1)
                if g >= 2 and h == 0:
                    act.wait_ge(t_stored[g % 2], 16 * BATCH * (g // 2))
                nc.scalar.activation(tst[0:2 * R, g % 2, h * HALF:(h + 1) * HALF], sbank[n % 2][0:2 * R],
                                     ACT.Copy).then_inc(t_made, 1)
            v_rows(0)
            for c, g in GROUPS[0]:
                prologue_quant(c, g)
            for n in range(STEPS):
                h, i = divmod(n, KT)
                for c, g in GROUPS[n + 1] if n + 1 < STEPS else []:
                    prologue_quant(c, g)
                if h == 0:
                    act.wait_ge(ufull, i + 1)
                    nc.scalar.activation(uall[:, :, i], sbank[i % 2][:, 0:BATCH * R].rearrange("p (b r) -> p b r", b=BATCH),
                                         ACT.Copy).then_inc(u_made, 1)
                if n + 1 < STEPS:
                    weight_hi(n + 1)
                if n == KT + 1:
                    gate_exp(0)
                if n == KT + 3:
                    gated_out(0)
                act.wait_ge(ofull, n + 1)
                nc.scalar.activation(p_hi[:, h, i], obank[n % RING], ACT.Copy).then_inc(p_hi_made, 1)
                if n == KT - 1:
                    kp_split(1)
                    v_rows(1)

            def x1_part(c, s, p):
                act.wait_ge(x1_made, c * PAIRS + p + 1)
                if not (isinstance(c, int) and c < 2):
                    act.wait_ge(ofull, STEPS + (c - 1) * KT)
                nc.scalar.activation(x1_hi[:, s, 2 * p:2 * p + 2], xbuf[:, s, 2 * p:2 * p + 2], ACT.Copy).then_inc(x1_hi_made, 1)

            TAKES = [[], [0], [1, 2], [3], [4, 5], [6], [7], []]

            def batch(t, u, quants, follows):
                b, s, _ = of_batch(t, u, 0)
                n, ns, _ = of_batch(t, u, 1)
                c, cs, ck = of_batch(t, u, 2)
                if quants:
                    act.wait_ge(xq_in[cs], 16 * (ck + 1))
                    levels(c, cs, 0)
                    quant(c, cs, ck, 0)
                for j in range(KT):
                    if j == 0:
                        act.wait_ge(zfull, b + 1)
                        if not (isinstance(b, int) and b == 0):
                            act.wait_ge(ofull, STEPS + b * KT)
                        nc.scalar.activation(zt, zbank[0:2 * R, 0:TOK], ACT.Copy).then_inc(zt_made, 1)
                        if quants:
                            magnitude(c, cs, ck)
                        if follows:
                            gate_exp(n)
                    if quants and j + 1 < G:
                        quant(c, cs, ck, j + 1)
                    if follows:
                        if j == 2:
                            gated_out(n)
                        if 3 <= j < 3 + PAIRS:
                            x1_part(n, ns, j - 3)
                    for m in TAKES[j]:
                        act.wait_ge(ofull, STEPS + b * KT + m + 1)
                        nc.scalar.activation(xbuf[:, s, m], obank[m % RING][:, 0:TOK], ACT.Identity,
                                             bias=bias[:, m:m + 1]).then_inc(ofree, 1)

            for p in range(PAIRS):
                x1_part(0, 0, p)
            with act.Fori(0, RINGS // 2) as t:
                for u in range(2):
                    batch(t, u, True, True)
            batch(RINGS // 2, 0, False, True)
            batch(RINGS // 2, 1, False, False)

        @block.vector
        def _(dve):
            def value(c, s, g):
                dve.wait_ge(raised, c * G + g + 1)
                v = val[:, turn(s, g)]
                nc.vector.tensor_scalar(v, v, width[:, g:g + 1], unshift[:, g:g + 1], ALU.min, ALU.add).then_inc(valued, 1)

            def mask(c, g):
                if g == 1:
                    dve.wait_ge(abs_made, c + 1)
                nc.vector.tensor_scalar(inside[:, g % 2], absx, thr[:, g - 1:g], None, ALU.is_le).then_inc(masked, 1)

            def before_merge(c, g):
                dve.wait_ge(valued, c * G + g + 1)
                dve.wait_ge(masked, c * (G - 1) + g)
                if g >= 2:
                    dve.wait_ge(merged, c * (G - 1) + g - 1)

            def merge(s, g):
                nc.vector.copy_predicated(val[:, acc(s)], inside[:, g % 2], val[:, turn(s, g)]).then_inc(merged, 1)

            def finish(c, s):
                dve.wait_ge(merged, (c + 1) * (G - 1))
                nc.vector.scalar_tensor_tensor(val[:, acc(s)], absx, thr[:, G - 1:G], val[:, acc(s)],
                                               ALU.is_gt, ALU.mult).then_inc(q_made, 1)

            def quant(c, s, g):
                value(c, s, g)
                if g:
                    before_merge(c, g)
                if g + 1 < G:
                    mask(c, g + 1)
                else:
                    nc.vector.memset(idle, 0.0)
                if g:
                    merge(s, g)
                if g + 1 == G:
                    finish(c, s)

            def weight_lo(n):
                dve.wait_ge(w_hi_made, n + 1)
                if n >= 2:
                    dve.wait_ge(ofull, n - 1)
                nc.vector.tensor_tensor(w_lo[n % 2], wst, w_hi[n % 2].bitcast(F32), ALU.subtract).then_inc(w_lo_made, 1)

            def k_add(h):
                for o in range(KT):
                    dve.wait_ge(kfull, h * KT + o + 1)
                    nc.vector.tensor_tensor(kst[:, o], sbank[o % 2], kst[:, o], ALU.add).then_inc(k_sum, 1)

            def kp_lo_part(h):
                for o in range(KT):
                    dve.wait_ge(kp_hi_made, h * KT + o + 1)
                    nc.vector.tensor_tensor(kp_lo[:, o], kst[:, o], kp_hi[:, o].bitcast(F32), ALU.subtract).then_inc(kp_lo_made, 1)

            dve.wait_ge(consts_in, 16 * N_CONST)
            nc.vector.tensor_tensor(gmix, gate_rep.unsqueeze(2).to_broadcast([P, BATCH, RG]),
                                    gsel.unsqueeze(1).to_broadcast([P, BATCH, RG]), ALU.mult).then_inc(gmix_made, 1)
            nc.vector.max(thr, par[:, 0])
            nc.vector.reciprocal(inv, par[:, 1])
            nc.vector.tensor_scalar(width, par[:, 1], LEVELS, None, ALU.mult)
            nc.vector.tensor_tensor(shift, par[:, 1], par[:, 2], ALU.mult).then_inc(table_step, 1)
            dve.wait_ge(table_step, 1)
            nc.vector.tensor_scalar(unshift, shift, -1.0, None, ALU.mult).then_inc(tables, 1)
            GATE_STEPS = 10
            def gate(c):
                done = [0]

                def then(ins):
                    done[0] += 1
                    ins.then_inc(gate_step, 1)
                    dve.wait_ge(gate_step, c * GATE_STEPS + done[0])

                mid = midbank[:, 0:TT * RT].rearrange("p (t m) -> p t m", t=TT)
                dve.wait_ge(mid_made, c + 1)
                then(nc.vector.tensor_copy(lg, mid[:, :, ER:RT]))
                then(nc.vector.reduce_max(best, lg, AX))
                nc.vector.tensor_tensor(gap, lg, best.unsqueeze(2).to_broadcast([P, TT, E]), ALU.subtract).then_inc(gap_made, 1)
                mine = lg.unsqueeze(3).to_broadcast([P, TT, E, E])
                other = lg.unsqueeze(2).to_broadcast([P, TT, E, E])
                then(nc.vector.tensor_tensor(ties, other, mine, ALU.is_equal))
                then(nc.vector.tensor_tensor(ties, ties, before, ALU.mult))
                then(nc.vector.tensor_tensor(beats, other, mine, ALU.is_gt))
                then(nc.vector.tensor_tensor(beats, beats, ties, ALU.add))
                then(nc.vector.reduce_sum(rank, beats, AX))
                dve.wait_ge(exp_made, c + 1)
                then(nc.vector.scalar_tensor_tensor(gates, rank, TOP_K, expo, ALU.is_lt, ALU.mult))
                then(nc.vector.reduce_sum(total, gates, AX))
                then(nc.vector.reciprocal(total, total))
                nc.vector.scalar_tensor_tensor(gates, gates, LORA0, total.unsqueeze(2).to_broadcast([P, TT, E]),
                                               ALU.mult, ALU.mult).then_inc(gate_scaled, 1)
                dve.wait_ge(gate_scaled, c + 1)
                nc.vector.tensor_tensor(mg.rearrange("p t (e r) -> p t e r", e=E), mid[:, :, 0:ER].rearrange("p t (e r) -> p t e r", e=E),
                                        gates.unsqueeze(3).to_broadcast([P, TT, E, R0]), ALU.mult).then_inc(mg_made, 1)

            def x1_sum(c, s, k, p):
                dve.wait_ge(dfull, c * PAIRS + p + 1)
                if p == 0:
                    dve.wait_ge(xbuf_in[s], 16 * (k + 1))
                pair = xbuf[:, s, 2 * p:2 * p + 2].rearrange("p k t -> p (k t)")
                nc.vector.tensor_tensor(pair, sbank[p % 2], pair, ALU.add).then_inc(x1_made, 1)

            def x1_part(c, s, p):
                dve.wait_ge(x1_hi_made, c * PAIRS + p + 1)
                nc.vector.tensor_tensor(x1_lo[:, s, 2 * p:2 * p + 2], xbuf[:, s, 2 * p:2 * p + 2],
                                        x1_hi[:, s, 2 * p:2 * p + 2].bitcast(F32), ALU.subtract).then_inc(x1_lo_made, 1)

            for c, g in AHEAD:
                quant(c, c, g)
            dve.wait_ge(k_in, 16)
            k_add(0)
            kp_lo_part(0)
            weight_lo(0)
            dve.wait_ge(cfull, 1)
            for q in range(BATCH // BG):
                last = nc.vector.scalar_tensor_tensor(cbd[:, q], misc[:, q * P:(q + 1) * P], LORA1, bdmask, ALU.mult, ALU.mult)
            last.then_inc(cbd_made, 1)
            for n in range(STEPS):
                h, i = divmod(n, KT)
                if n == KT - 1:
                    dve.wait_ge(k_in, 32)
                    k_add(1)
                for c, g in GROUPS[n]:
                    quant(c, c, g)
                if n == KT + 1:
                    gate(0)
                if n + 1 < STEPS and n + 1 != KT:
                    weight_lo(n + 1)
                dve.wait_ge(p_hi_made, n + 1)
                nc.vector.tensor_tensor(p_lo[:, h, i], obank[n % RING], p_hi[:, h, i].bitcast(F32), ALU.subtract).then_inc(ofree, 1)
                if n == KT - 1:
                    weight_lo(KT)
                    kp_lo_part(1)

            for p in range(PAIRS):
                x1_sum(0, 0, 0, p)
                x1_part(0, 0, p)

            def batch(t, u, quants, follows):
                n, ns, nk = of_batch(t, u, 1)
                c, cs, _ = of_batch(t, u, 2)
                for j in range(KT):
                    if follows:
                        if 3 <= j < 3 + PAIRS:
                            x1_sum(n, ns, nk, j - 3)
                        if 4 <= j < 4 + PAIRS:
                            x1_part(n, ns, j - 4)
                    if quants:
                        quant(c, cs, j)
                    if follows and j == 0:
                        gate(n)

            with dve.Fori(0, RINGS // 2) as t:
                for u in range(2):
                    batch(t, u, True, True)
            batch(RINGS // 2, 0, False, True)

        @block.tensor
        def _(pe):
            mm = nc.tensor.matmul
            gm = gmix.rearrange("p b r -> p (b r)")
            pe.wait_ge(gmix_made, 1)
            pe.wait_ge(lora_in, 16)
            for o in range(KT):
                if o >= 2:
                    pe.wait_ge(sfree, o - 1)
                for g in range(NG):
                    last = mm(sbank[o % 2][:, g * BATCH * RG:(g + 1) * BATCH * RG], la[:, g, o * P:(o + 1) * P], gm, start=True, stop=True)
                last.then_inc(sfull, 1)

            def k_update(h):
                for o in range(KT):
                    if o >= 2:
                        pe.wait_ge(k_sum, h * KT + o - 1)
                    elif h == 0:
                        pe.wait_ge(sfree, KT - 1 + o)
                    else:
                        pe.wait_ge(u_made, KT - 1 + o)
                    mm(sbank[o % 2], tst[2 * R:3 * R, 0, o * P:(o + 1) * P], tst[2 * R:3 * R, 1, h * HALF:(h + 1) * HALF],
                       start=True, stop=True).then_inc(kfull, 1)

            def v_product(h):
                pe.wait_ge(k_sum, (h + 1) * KT)
                if h == 0:
                    pe.wait_ge(cbd_made, 1)
                else:
                    pe.wait_ge(v_made, 1)
                for o in range(KT):
                    last = mm(misc, bw[:, o], kst[:, o], start=o == 0, stop=o == KT - 1)
                last.then_inc(vfull, 1)

            pe.wait_ge(shared_in, 48)
            k_update(0)
            pe.wait_ge(sfree, KT)
            for o in range(KT):
                last = mm(misc[:, 0:BATCH * R], bw[:, o], aefft[:, o], start=o == 0, stop=o == KT - 1)
            last.then_inc(cfull, 1)
            pe.wait_ge(lb_in, 16)
            for n in range(NG * HALVES):
                g, h = divmod(n, HALVES)
                if n < 2:
                    pe.wait_ge(k_sum, KT - 1 + n)
                else:
                    pe.wait_ge(t_made, n - 1)
                mm(sbank[n % 2][0:2 * R], gm, lb[:, g, h * HALF:(h + 1) * HALF], start=True, stop=True).then_inc(sfull, 1)
            v_product(0)
            pe.wait_ge(ra_in, 32)

            def mid(c, s):
                pe.wait_ge(q_made, c + 1)
                if not (isinstance(c, int) and c == 0):
                    pe.wait_ge(mg_made, c)
                for t in range(TT):
                    for k in range(KT):
                        last = mm(midbank[:, t * RT:(t + 1) * RT], val[:, acc(s), k, t * P:(t + 1) * P], ra[:, k],
                                  start=k == 0, stop=k == KT - 1)
                last.then_inc(mid_made, 1)

            def gated_turn(c):
                pe.wait_ge(mg_made, c + 1)
                if not (isinstance(c, int) and c == 0):
                    pe.wait_ge(mgt_made, c)
                for t in range(TT):
                    last = mm(mgbank[0:ER, t * P:(t + 1) * P], mg[:, t], ident.bitcast(F32), start=True, stop=True)
                last.then_inc(mgt_full, 1)

            def layer0(c, p):
                pe.wait_ge(mgt_made, c + 1)
                if not (isinstance(c, int) and c == 0 and p < 2):
                    pe.wait_ge(x1_made, c * PAIRS + p - 1)
                for k in (2 * p, 2 * p + 1):
                    last = mm(sbank[p % 2][:, k % 2 * TOK:(k % 2 + 1) * TOK], ber[:, k * P:(k + 1) * P], mgt, start=True, stop=True)
                last.then_inc(dfull, 1)

            pe.wait_ge(alt_in, 16 * BATCH)
            for n in range(STEPS):
                h, i = divmod(n, KT)
                if h == 0:
                    pe.wait_ge(w_in, 16 * (n + 1))
                    if i < 2:
                        pe.wait_ge(t_made, NG * HALVES - 1 + i)
                    else:
                        pe.wait_ge(u_made, i - 1)
                    for o in range(KT):
                        mm(sbank[i % 2][:, 0:BATCH * R], wst[:, o], aefft[:, o], start=o == 0, stop=False)
                    for q in range(BATCH // BG):
                        last = mm(sbank[i % 2][:, q * P:(q + 1) * P], alt[:, q, i * P:(i + 1) * P], cbd[:, q],
                                  start=False, stop=q == BATCH // BG - 1)
                    last.then_inc(ufull, 1)
                if n == KT - 1:
                    k_update(1)
                pe.wait_ge(w_lo_made, n + 1)
                if n >= RING:
                    pe.wait_ge(ofree, n - RING + 1)
                for o in range(KT):
                    if i == 0:
                        pe.wait_ge(kp_lo_made, h * KT + o + 1)
                    mm(obank[n % RING], w_hi[n % 2][:, o], kp_hi[:, o], start=o == 0, stop=False)
                    mm(obank[n % RING], w_hi[n % 2][:, o], kp_lo[:, o], start=False, stop=False)
                    last = mm(obank[n % RING], w_lo[n % 2][:, o], kp_hi[:, o], start=False, stop=o == KT - 1)
                last.then_inc(ofull, 1)
                if n == KT - 1:
                    v_product(1)
                if n == MID0:
                    mid(0, 0)
                if n == KT + 2:
                    pe.wait_ge(ident_made, 1)
                    gated_turn(0)
            for p in range(PAIRS):
                layer0(0, p)

            def batch(t, u, follows):
                b, s, sk = of_batch(t, u, 0)
                n, ns, _ = of_batch(t, u, 1)
                pe.wait_ge(x1_made, (b + 1) * PAIRS)
                pe.wait_ge(ub_in[s], 32 * (sk + 1))
                for k in range(KT):
                    last = mm(zbank[0:2 * R, 0:TOK], ub[:, s, k], xbuf[:, s, k], start=k == 0, stop=k == KT - 1)
                last.then_inc(zfull, 1)
                if follows:
                    mid(n, ns)
                pe.wait_ge(x1_lo_made, (b + 1) * PAIRS)
                for j in range(KT):
                    h, at = j // (KT // 2), j % (KT // 2) * P
                    pe.wait_ge(ofree, STEPS + b * KT + j - RING + 1)
                    o = obank[j % RING][:, 0:TOK]
                    for k in range(KT):
                        mm(o, p_hi[:, h, k, at:at + P], x1_hi[:, s, k], start=k == 0, stop=False)
                        mm(o, p_hi[:, h, k, at:at + P], x1_lo[:, s, k], start=False, stop=False)
                        mm(o, p_lo[:, h, k, at:at + P], x1_hi[:, s, k], start=False, stop=False)
                    mm(o, ident, x1_hi[:, s, j], start=False, stop=False)
                    mm(o, ident, x1_lo[:, s, j], start=False, stop=False)
                    if j == 0:
                        pe.wait_ge(zt_made, b + 1)
                        pe.wait_ge(tb_in[s], 16 * (sk + 1))
                    mm(o, tb[:, s, j * P:(j + 1) * P], zt, start=False, stop=True).then_inc(ofull, 1)
                    if follows:
                        if j == 1:
                            gated_turn(n)
                        if 2 <= j < 2 + PAIRS:
                            layer0(n, j - 2)

            with pe.Fori(0, RINGS // 2) as t:
                for u in range(2):
                    batch(t, u, True)
            batch(RINGS // 2, 0, True)
            batch(RINGS // 2, 1, False)


def kernel(**inputs):
    import concourse.bacc as bacc
    from concourse.bass_utils import run_bass_kernel_spmd

    v = {k: np.asarray(x) for k, x in inputs.items()}
    c = np.ascontiguousarray
    i4, i16 = np.arange(E), np.arange(P)
    before = np.broadcast_to((i4[None, :] < i4[:, None]).astype(np.float32), (P, TT, E, E))
    arrays = {
        "xt": c(v["x"].reshape(BATCH * TOK, D).T),
        "par": c(np.broadcast_to(np.stack([v["condB_thresholds"], v["condB_deltas"], v["condB_zeropoints"]]), (P, 3, G))),
        "ra": c(np.concatenate([v["L0_ffn_A"].reshape(ER, D), v["L0_ffn_router_w"]]).reshape(RT, KT, P).transpose(2, 1, 0)),
        "ber": c(v["L0_ffn_B"].transpose(0, 2, 1).reshape(ER, D)),
        "w": c(v["L1_cond_W"]),
        "k": c(v["L1_ffn_kernel"]),
        "as": c(v["L1_ffn_lora_A_shared"]),
        "bst": c(v["L1_ffn_lora_B_shared"].T),
        "la": c(v["L1_ffn_lora_A"].transpose(1, 0, 2).reshape(NG, P, D).transpose(1, 0, 2)),
        "lb": c(v["L1_ffn_lora_B"].transpose(2, 0, 1).reshape(NG, P, D).transpose(1, 0, 2)),
        "gate_rep": c(np.tile(v["L1_ffn_gate"].T, (RG, 1))),
        "bw": c(np.tile(v["L1_cond_lora_B_w"].reshape(KT, P, R).transpose(1, 0, 2), (1, 1, BG))),
        "al": c(v["L1_cond_lora_A"].reshape(LAB, KT, P, R).transpose(0, 2, 1, 3)),
        "alt": c(v["L1_cond_lora_A"].transpose(0, 2, 1)),
        "bias": c(v["L1_ffn_bias"].reshape(KT, P).T),
        "gsel": (i16[:, None] // NL == np.arange(RG)[None, :]).astype(np.float32),
        "bdmask": (i16[:, None] // R == i16[None, :] // R).astype(np.float32),
        "ident": np.eye(P, dtype=np.float32),
        "before": c(before),
        "itok": c(v["itok_B_0_2"].reshape(1, BATCH)),
    }
    nc = bacc.Bacc("TRN2", target_bir_lowering=False, num_devices=1)
    aps = {k: nc.dram_tensor(f"{k}_in", x.shape, mybir.dt.from_np(x.dtype), kind="ExternalInput").ap() for k, x in arrays.items()}
    out_t = nc.dram_tensor("out_t", (D, BATCH * TOK), F32, kind="ExternalOutput").ap()
    itok = aps.pop("itok")
    build(nc, aps, out_t, itok)
    r = run_bass_kernel_spmd(nc, [{f"{k}_in": x for k, x in arrays.items()}], core_ids=[0])
    return c(r.results[0]["out_t"].T).reshape(BATCH, TOK, D)
```

```python
import numpy as np
import concourse.bass as bass
from concourse import mybir

F32 = mybir.dt.float32
F32R = mybir.dt.float32r
I16 = mybir.dt.int16
I32 = mybir.dt.int32
U8 = mybir.dt.uint8
ALU = mybir.AluOpType
ACT = mybir.ActivationFunctionType
AX = mybir.AxisListType.X

P = 128
BATCH = 8
TOK = 256
TT = TOK // P
D = 1024
KT = D // P
G = 8
E, R0 = 4, 16
ER = E * R0
RT = ER + E
R = 32
NL = 16
RG = P // NL
NG = R // RG
LAB = 5
HALF = D // 2
HALVES = 2
STEPS = HALVES * KT
BG = P // R
LEVELS = 63.0
TOP_K = 2.0
ZSLOTS = 3
LORA0 = 4.0
LORA1 = 0.5


def build(nc, a, out_t, itok):
    arena = [(nc.sbuf_base + 31) // 32 * 32]

    def place(name, shape, dt, at=None, after=0):
        size = int(np.prod(shape[1:])) * mybir.dt.size(dt)
        size = (size + 31) // 32 * 32
        if at is None:
            at = arena[0]
            arena[0] += size
        t = nc.alloc_sbuf_tensor_at(name, shape, dt, offset=at + after)
        return t[:], at

    p_hi, _ = place("p_hi", [P, HALVES, KT, HALF], F32R)
    p_lo, p_lo_at = place("p_lo", [P, HALVES, KT, HALF], F32R)
    p_hi_at = p_lo_at - HALVES * KT * HALF * 4
    half_bytes = KT * HALF * 4
    val, _ = place("val", [P, 3, KT, TOK], F32)
    absx, _ = place("absx", [P, KT, TOK], F32)
    level, _ = place("level", [P, 2, KT, TOK], I16)
    inside, _ = place("inside", [P, 2, KT, TOK], U8)
    xq, _ = place("xq", [P, 2, KT, TOK], F32)
    xbuf, xbuf_at = place("xbuf", [P, 2, KT, TOK], F32)
    x_hi, x_hi_at = place("x_hi", [P, 2, KT, TOK], F32R)
    x_lo, x_lo_at = place("x_lo", [P, 2, KT, TOK], F32R)
    ub, ub_at = place("ub", [P, 2, KT, 2 * R], F32)
    tb, tb_at = place("tb", [P, 2, D], F32)
    uall, _ = place("uall", [P, BATCH, KT, R], F32)
    ra, _ = place("ra", [P, KT, RT], F32)
    bet, bet_at = place("bet", [P, KT, 2 * ER], F32)
    mg, _ = place("mg", [P, TT, 2 * ER], F32)
    zt, zt_at = place("zt", [P, ZSLOTS, TOK], F32)
    ident, _ = place("ident", [P, P], F32R)
    bias, _ = place("bias", [P, KT], F32)
    par, _ = place("par", [P, 3, G], F32)
    thr, _ = place("thr", [P, G], F32)
    inv, _ = place("inv", [P, G], F32)
    shift, _ = place("shift", [P, G], F32)
    unshift, _ = place("unshift", [P, G], F32)
    width, _ = place("width", [P, G], F32)
    before, _ = place("before", [P, TT, E, E], F32)
    lg, _ = place("lg", [P, TT, E], F32)
    beats, _ = place("beats", [P, TT, E, E], F32)
    ties, _ = place("ties", [P, TT, E, E], F32)
    rank, _ = place("rank", [P, TT, E], F32)
    best, _ = place("best", [P, TT], F32)
    gap, _ = place("gap", [P, TT, E], F32)
    expo, _ = place("expo", [P, TT, E], F32)
    gates, _ = place("gates", [P, TT, E], F32)
    total, _ = place("total", [P, TT], F32)
    itok_sb, _ = place("itok_sb", [1, BATCH], I32)
    gate_rep, _ = place("gate_rep", [P, BATCH], F32)
    gsel, _ = place("gsel", [P, RG], F32)
    gmix, _ = place("gmix", [P, RG, BATCH], F32)
    la, _ = place("la", [P, NG, D], F32, p_hi_at)
    lb, _ = place("lb", [P, NG, D], F32, p_lo_at)
    kst, _ = place("kst", [P, KT, HALF], F32, p_hi_at, half_bytes)
    aefft, _ = place("aefft", [P, KT, BATCH * R], F32, p_lo_at, half_bytes)
    alt, _ = place("alt", [P, BATCH // BG, D], F32, p_lo_at, half_bytes + KT * BATCH * R * 4)
    kp_hi, _ = place("kp_hi", [P, KT, HALF], F32R, x_hi_at)
    kp_lo, _ = place("kp_lo", [P, KT, HALF], F32R, x_lo_at)
    w_bytes = KT * P * 4
    w_hi = [place(f"w_hi{i}", [P, KT, P], F32R, xbuf_at, 2 * i * w_bytes)[0] for i in range(2)]
    w_lo = [place(f"w_lo{i}", [P, KT, P], F32R, xbuf_at, (2 * i + 1) * w_bytes)[0] for i in range(2)]
    wst = [place(f"wst{i}", [P, KT, P], F32, at)[0] for i, at in enumerate((ub_at, bet_at))]
    ident_raw, _ = place("ident_raw", [P, P], F32, zt_at)
    tst, _ = place("tst", [P, 2, D], F32, tb_at)
    bw, bw_at = place("bw", [P, KT, P], F32)
    bu, _ = place("bu", [P, 2, 2 * R], F32, bw_at)
    cbd, _ = place("cbd", [P, BATCH // BG, P], F32, zt_at, TOK * 4)
    bdmask, _ = place("bdmask", [P, P], F32, zt_at, P * 4)
    bet_hi, _ = place("bet_hi", [P, KT, 2 * ER], F32R, xbuf_at, KT * TOK * 4)
    bet_lo, _ = place("bet_lo", [P, KT, 2 * ER], F32R, xbuf_at, KT * TOK * 4 + KT * 2 * ER * 4)
    assert arena[0] <= nc.sbuf_usable_end, (arena[0], nc.sbuf_usable_end)
    t_dram = nc.dram_tensor("t_dram", (R, BATCH, D), F32).ap()

    bank = [nc.alloc_psum_tensor(f"bank{i}", [P, HALF], F32)[:] for i in range(8)]
    obank, sbank, cols = bank[0:4], bank[4:6], bank[0:6]
    zbank, midbank = bank[6], bank[7]
    misc, cbank = zbank, midbank
    mgbank = midbank[:, HALF // 2:HALF]

    sem = nc.alloc_semaphore
    consts_in, lb_in, shared_in, bw_in, itok_in, alt_in, ra_in = (
        sem(n) for n in ("consts_in", "lb_in", "shared_in", "bw_in", "itok_in", "alt_in", "ra_in"))
    xq_in = [sem("xq_in0"), sem("xq_in1")]
    k_in, w_in, bet_in = sem("k_in"), [sem("w_in0"), sem("w_in1")], sem("bet_in")
    lora_in = [sem(f"lora_in{g}") for g in range(NG)]
    par_in, mix_in = sem("par_in"), sem("mix_in")
    xbuf_in = [sem("xbuf_in0"), sem("xbuf_in1")]
    ub_in = [sem("ub_in0"), sem("ub_in1")]
    tb_in = [sem("tb_in0"), sem("tb_in1")]
    t_stored, v_moved = [sem("t_stored0"), sem("t_stored1")], sem("v_moved")
    out_stored = [sem("out_stored0"), sem("out_stored1")]
    ident_made = sem("ident_made")
    tables, table_step, gmix_made = sem("tables"), sem("table_step"), sem("gmix_made")
    afull, afree, tfull = sem("afull"), sem("afree"), sem("tfull")
    cfull, cbd_made = sem("cfull"), sem("cbd_made")
    vfull, v_made = sem("vfull"), sem("v_made")
    t_made = sem("t_made")
    kfull, k_sum, kp_hi_made, kp_lo_made = sem("kfull"), sem("k_sum"), sem("kp_hi_made"), sem("kp_lo_made")
    w_hi_made, w_lo_made = sem("w_hi_made"), sem("w_lo_made")
    ufull, u_made = sem("ufull"), sem("u_made")
    ofull, p_hi_made, ofree = sem("ofull"), sem("p_hi_made"), sem("ofree")
    abs_made, levels_made, raised = sem("abs_made"), sem("levels_made"), sem("raised")
    valued, masked, merged, q_made = sem("valued"), sem("masked"), sem("merged"), sem("q_made")
    mid_made, gate_step, gap_made, exp_made = sem("mid_made"), sem("gate_step"), sem("gap_made"), sem("exp_made")
    gates_made = sem("gates_made")
    mg_made, mgt_full, mgt_made = sem("mg_made"), sem("mgt_full"), sem("mgt_made")
    x_hi_made, x_lo_made = sem("x_hi_made"), sem("x_lo_made")
    bet_hi_made, bet_lo_made, bpfull, bp_made = sem("bet_hi_made"), sem("bet_lo_made"), sem("bpfull"), sem("bp_made")
    mg_zeroed = sem("mg_zeroed")
    bufull, bu_made = sem("bufull"), sem("bu_made")
    zfull, zt_made = sem("zfull"), sem("zt_made")

    XPARTS = 2
    XK = KT // XPARTS
    RING = len(obank)
    CRING = len(cols)
    N_CONST = 4

    AHEAD = 5
    TAKEN = [1, 1, 2, 1, 1, 1, 2, 1, 2, 1, 0, 1, 0, 1, 0, 1, 1, 1]
    ORDER = [(c, g) for c in range(BATCH) for g in range(G)]
    SLOTS = STEPS + BATCH * KT
    LAST = STEPS + BATCH * KT - 8
    rest, room = len(ORDER) - AHEAD - sum(TAKEN), LAST + 1 - len(TAKEN)
    TAKEN += [(i + 1) * rest // room - i * rest // room for i in range(room)]
    TAKEN += [0] * (SLOTS - len(TAKEN))
    starts = [AHEAD + sum(TAKEN[:i]) for i in range(SLOTS + 1)]
    GROUPS = [ORDER[starts[i]:starts[i + 1]] for i in range(SLOTS)] + [[]]
    DONE = [max([-1] + [i for i in range(SLOTS) if (c, G - 1) in GROUPS[i]]) for c in range(BATCH)]
    MID = {d + 1: c for c, d in enumerate(DONE)}
    RANK = {d + 2: c for c, d in enumerate(DONE)}
    GATE = {d + 3: c for c, d in enumerate(DONE)}
    TURN = {d + 4: c for c, d in enumerate(DONE)}
    OUT = {d + 5 if c < ZSLOTS else max(d + 5, STEPS + (c - ZSLOTS + 1) * KT): c for c, d in enumerate(DONE)}
    OUT_AT = {c: k for k, c in OUT.items()}
    XAT, ZAT = (4, 6), 6
    CLOSE = [0 if OUT_AT[b] < STEPS + b * KT else max(1, OUT_AT[b] - STEPS - b * KT) for b in range(BATCH)]
    ZOUT = [b * KT + (CLOSE[b] + 1 if CLOSE[b] else 0) for b in range(BATCH)]
    LAG = 2
    TAKE = [max(q + LAG, ZOUT[q // KT]) for q in range(BATCH * KT)]

    def slot(b, j):
        return STEPS + b * KT + j

    def acc(c):
        return c % 2

    def turn(c, g):
        return acc(c) if g == 0 else 2 if g % 2 else 1 - acc(c)

    x_v = a["xt"].rearrange("(k p) t -> p k t", p=P)
    out_v = out_t.rearrange("(k p) t -> p k t", p=P)
    w_v = a["w"].rearrange("(o p) (i c) -> i p o c", p=P, c=P)
    k_v = a["k"].rearrange("(o p) (h c) -> h p o c", p=P, c=HALF)

    with nc.allow_non_contiguous_dma(reason="rows of 1 KB and small constants"), nc.Block() as block:

        @block.gpsimd
        def _(pool):
            for c in range(BATCH):
                if c == 1:
                    pool.wait_ge(k_in, 16)
                if c >= 2:
                    pool.wait_ge(levels_made, (c - 1) * G)
                    pool.wait_ge(abs_made, c - 1)
                pool.dma_start(xq[:, c % 2], x_v[:, :, c * TOK:(c + 1) * TOK]).then_inc(xq_in[c % 2], 16)

        @block.sync
        def _(sp):
            sp.dma_start(par, a["par"]).then_inc(par_in, 16)
            sp.dma_start(gate_rep, a["gate_rep"]).then_inc(mix_in, 16)
            sp.dma_start(gsel, a["gsel"]).then_inc(mix_in, 16)
            for g in range(NG):
                sp.dma_start(la[:, g], a["la"][:, g]).then_inc(lora_in[g], 16)
            sp.dma_start(tst[2 * R:3 * R, 0], a["as"]).then_inc(shared_in, 16)
            sp.dma_start(tst[2 * R:3 * R, 1], a["bst"]).then_inc(shared_in, 16)
            sp.dma_start(kst, k_v[0]).then_inc(k_in, 16)
            for dst, name in ((bdmask, "bdmask"), (ident_raw, "ident"), (before, "before"), (bias, "bias")):
                sp.dma_start(dst, a[name]).then_inc(consts_in, 16)
            sp.dma_start(itok_sb, itok).then_inc(itok_in, 16)
            sp.dma_start(bw, a["bw"]).then_inc(bw_in, 16)
            sp.dma_start(wst[0], w_v[0]).then_inc(w_in[0], 16)
            sp.dma_start(ra, a["ra"]).then_inc(ra_in, 16)
            sp.dma_start(lb, a["lb"]).then_inc(lb_in, 16)
            sp.wait_ge(itok_in, 16)
            label = [sp.value_load(itok_sb[0:1, b:b + 1], min_val=0, max_val=LAB - 1) for b in range(BATCH)]
            for b in range(BATCH):
                sp.dma_start(alt[b % BG * R:(b % BG + 1) * R, b // BG],
                             a["alt"][bass.ds(label[b], 1)].rearrange("o r i -> (o r) i")).then_inc(alt_in, 16)
            sp.dma_start(wst[1], w_v[1]).then_inc(w_in[1], 16)
            sp.wait_ge(kp_hi_made, KT)
            sp.wait_ge(kp_lo_made, KT)
            sp.wait_ge(vfull, 1)
            sp.dma_start(kst, k_v[1]).then_inc(k_in, 16)
            for g in range(NG):
                sp.wait_ge(t_made, 2 * (g + 1))
                sp.dma_start(t_dram[g * RG:(g + 1) * RG].rearrange("r b d -> (r b) d"), tst[0:2 * R, g % 2]).then_inc(t_stored[g % 2], 16)

            def adapters(b):
                s = b % 2
                sp.dma_start(ub[:, s, :, 0:R], uall[:, b]).then_inc(ub_in[s], 16)
                sp.dma_start(ub[:, s, :, R:2 * R], a["al"][bass.ds(label[b], 1)].rearrange("o p k r -> p (o k) r")).then_inc(ub_in[s], 16)

            def rows(b):
                sp.dma_start(tb[0:R, b % 2], t_dram[:, b]).then_inc(tb_in[b % 2], 16)

            for n in range(2, STEPS):
                sp.wait_ge(w_hi_made, n - 1)
                sp.wait_ge(w_lo_made, n - 1)
                sp.wait_ge(ufull, min(n - 1, KT))
                sp.dma_start(wst[n % 2], w_v[n % KT]).then_inc(w_in[n % 2], 16)
                if n == KT + 2:
                    for s in range(2):
                        sp.wait_ge(t_stored[s], 16 * NG // 2)
                    sp.wait_ge(kfull, HALVES * KT)
                    sp.wait_ge(v_made, HALVES)
                    for s in range(2):
                        sp.dma_start(tb[R:2 * R, s], tst[3 * R:4 * R, 0]).then_inc(v_moved, 16)
                        rows(s)
            sp.wait_ge(u_made, KT)
            for b in range(2):
                if b == 0:
                    sp.wait_ge(w_hi_made, STEPS - 1)
                    sp.wait_ge(w_lo_made, STEPS - 1)
                adapters(b)
            sp.wait_ge(w_hi_made, STEPS)
            sp.wait_ge(w_lo_made, STEPS)
            sp.dma_start(bet, a["bet"]).then_inc(bet_in, 16)
            sp.wait_ge(ofull, STEPS - 1)
            sp.dma_start(xbuf[:, 0], x_v[:, :, 0:TOK]).then_inc(xbuf_in[0], 16)
            sp.wait_ge(bpfull, HALVES)
            sp.dma_start(xbuf[:, 1], x_v[:, :, TOK:2 * TOK]).then_inc(xbuf_in[1], 16)

            for b in range(BATCH):
                for h in range(HALVES):
                    sp.wait_ge(ofree, STEPS + b * KT + (h + 1) * KT // 2)
                    half = slice(h * KT // 2, (h + 1) * KT // 2)
                    sp.dma_start(out_v[:, half, b * TOK:(b + 1) * TOK], xbuf[:, b % 2, half]).then_inc(out_stored[h], 16)
                    if b + 2 < BATCH:
                        if h == 0:
                            sp.wait_ge(zfull, b + 1)
                            adapters(b + 2)
                        else:
                            rows(b + 2)
                        sp.wait_ge(out_stored[h], 16 * (b + 1))
                        sp.dma_start(xbuf[:, b % 2, half], x_v[:, half, (b + 2) * TOK:(b + 3) * TOK]).then_inc(xbuf_in[b % 2], 16)
            for h in range(HALVES):
                sp.wait_ge(out_stored[h], 16 * BATCH)

        @block.scalar
        def _(act):
            def magnitude(c):
                if c:
                    act.wait_ge(q_made, c)
                nc.scalar.activation(absx, xq[:, c % 2], ACT.Abs).then_inc(abs_made, 1)

            def levels(c, g):
                if g == 0:
                    act.wait_ge(xq_in[c % 2], 16 * (c // 2 + 1))
                if c * G + g >= 2:
                    act.wait_ge(raised, c * G + g - 1)
                nc.scalar.activation(level[:, g % 2], xq[:, c % 2], ACT.Copy, scale=inv[:, g:g + 1]).then_inc(levels_made, 1)

            def raise_levels(c, g):
                act.wait_ge(levels_made, c * G + g + 1)
                if c and g == 2:
                    act.wait_ge(mid_made, c)
                elif g >= 3:
                    act.wait_ge(merged, c * (G - 1) + g - 2)
                elif c and g == 1:
                    act.wait_ge(merged, c * (G - 1))
                elif c and g == 0:
                    act.wait_ge(merged, c * (G - 1) - 1)
                nc.scalar.activation(val[:, turn(c, g)], level[:, g % 2], ACT.Relu, bias=shift[:, g:g + 1],
                                     scale=par[:, 1, g:g + 1]).then_inc(raised, 1)

            def quant(c, g):
                if c == 0 and g == 0:
                    levels(0, 0)
                    magnitude(0)
                if c and g == 1:
                    magnitude(c)
                if g + 1 < G:
                    levels(c, g + 1)
                elif c + 1 < BATCH:
                    levels(c + 1, 0)
                raise_levels(c, g)

            def weight_hi(n):
                act.wait_ge(w_in[n % 2], 16 * (n // 2 + 1))
                if n >= 2:
                    act.wait_ge(ofull, n - 1)
                nc.scalar.activation(w_hi[n % 2], wst[n % 2], ACT.Copy).then_inc(w_hi_made, 1)

            def kp_split(h):
                for o in range(KT):
                    act.wait_ge(k_sum, h * KT + o + 1)
                    if h == 1 and o == 0:
                        act.wait_ge(ofull, KT)
                    nc.scalar.activation(kp_hi[:, o], kst[:, o], ACT.Copy).then_inc(kp_hi_made, 1)

            def v_rows(h):
                act.wait_ge(vfull, h + 1)
                nc.scalar.activation(tst[3 * R:4 * R, 0, h * HALF:(h + 1) * HALF], misc[3 * R:4 * R], ACT.Copy,
                                     scale=LORA1).then_inc(v_made, 1)

            def gate_exp(c):
                act.wait_ge(gap_made, c + 1)
                nc.scalar.activation(expo, gap, ACT.Exp).then_inc(exp_made, 1)

            def gated_out(c):
                act.wait_ge(mgt_full, c + 1)
                if c >= ZSLOTS:
                    act.wait_ge(ofull, STEPS + (c - ZSLOTS + 1) * KT)
                nc.scalar.activation(zt[2 * R:P, c % ZSLOTS], mgbank[ER:2 * ER, 0:TOK], ACT.Copy).then_inc(mgt_made, 1)

            def x_part(c, p):
                act.wait_ge(xbuf_in[c % 2], 16 + 32 * (c // 2))
                act.wait_ge(ofull, STEPS + max(c - 1, 0) * KT)
                part = slice(p * XK, (p + 1) * XK)
                nc.scalar.activation(x_hi[:, c % 2, part], xbuf[:, c % 2, part], ACT.Copy).then_inc(x_hi_made, 1)

            def bu_out(c):
                act.wait_ge(bufull, c + 1)
                if c >= 2:
                    act.wait_ge(zfull, c - 1)
                nc.scalar.activation(bu[2 * R:P, c % 2], zbank[ER:2 * ER, TOK:TOK + 2 * R], ACT.Copy).then_inc(bu_made, 1)

            def bp_out(s):
                for h in range(HALVES):
                    act.wait_ge(bpfull, h + 1)
                    act.wait_ge(v_moved, 32)
                    nc.scalar.activation(tb[2 * R:P, s, h * HALF:(h + 1) * HALF], sbank[h][ER:2 * ER], ACT.Copy).then_inc(bp_made, 1)

            def rows_out(n):
                g, h = divmod(n, HALVES)
                act.wait_ge(tfull, n + 1)
                if g >= 2 and h == 0:
                    act.wait_ge(t_stored[g % 2], 16 * (g // 2))
                nc.scalar.activation(tst[0:2 * R, g % 2, h * HALF:(h + 1) * HALF], obank[n % RING][0:2 * R],
                                     ACT.Copy).then_inc(t_made, 1)

            act.wait_ge(tables, 1)
            quant(*ORDER[0])
            for m in range(KT // 2):
                act.wait_ge(afull, m + 1)
                for i in range(2):
                    last = nc.scalar.activation(
                        aefft[:, 2 * m + i].rearrange("p (b g r) -> p b g r", b=BATCH, g=NG),
                        obank[m][:, i * BATCH * R:(i + 1) * BATCH * R].rearrange("p (g r b) -> p b g r", g=NG, b=BATCH), ACT.Copy)
                last.then_inc(afree, 1)
            kp_split(0)
            weight_hi(0)
            act.wait_ge(consts_in, 16 * N_CONST)
            nc.scalar.activation(ident, ident_raw, ACT.Copy).then_inc(ident_made, 1)
            quant(*ORDER[1])
            quant(*ORDER[2])
            v_rows(0)
            weight_hi(1)
            for n in range(NG * HALVES):
                rows_out(n)
                if n in (NG - 1, NG * HALVES - 1):
                    quant(*ORDER[3 + n // NG])
            for c, g in GROUPS[0]:
                quant(c, g)
            def p_out(n):
                act.wait_ge(ofull, n + 1)
                h, i = divmod(n, KT)
                nc.scalar.activation(p_hi[:, h, i], obank[n % RING], ACT.Copy).then_inc(p_hi_made, 1)

            for n in range(STEPS):
                if n == KT:
                    kp_split(1)
                if n and n + 1 < STEPS:
                    weight_hi(n + 1)
                if n < KT:
                    act.wait_ge(ufull, n + 1)
                    nc.scalar.activation(uall[:, :, n], sbank[n % 2][:, 0:BATCH * R].rearrange("p (b r) -> p b r", b=BATCH),
                                         ACT.Copy).then_inc(u_made, 1)
                if n:
                    p_out(n - 1)
                if n == KT:
                    v_rows(1)
                if n in OUT:
                    gated_out(OUT[n])
                for c, g in GROUPS[n + 1]:
                    quant(c, g)
                if n in RANK:
                    gate_exp(RANK[n])
            act.wait_ge(ofull, STEPS)
            act.wait_ge(bet_in, 16)
            nc.scalar.activation(bet_hi, bet, ACT.Copy).then_inc(bet_hi_made, 1)
            p_out(STEPS - 1)

            bu_out(0)
            for p in range(XPARTS):
                x_part(0, p)
            bp_out(0)
            for q in range(BATCH * KT + LAG):
                b, j = divmod(q, KT)
                if q in ZOUT:
                    z = ZOUT.index(q)
                    act.wait_ge(zfull, z + 1)
                    if z >= ZSLOTS:
                        act.wait_ge(ofull, STEPS + (z - ZSLOTS + 1) * KT)
                    nc.scalar.activation(zt[0:2 * R, z % ZSLOTS], zbank[0:2 * R, 0:TOK], ACT.Copy).then_inc(zt_made, 1)
                if q == 1:
                    bp_out(1)
                if slot(b, j) in OUT:
                    gated_out(OUT[slot(b, j)])
                if b < BATCH:
                    for c, g in GROUPS[slot(b, j) + 1]:
                        quant(c, g)
                for m in range(BATCH * KT):
                    if TAKE[m] == q:
                        act.wait_ge(ofull, STEPS + m + 1)
                        nc.scalar.activation(xbuf[:, m // KT % 2, m % KT], cols[m % CRING][:, 0:TOK], ACT.Identity,
                                             bias=bias[:, m % KT:m % KT + 1]).then_inc(ofree, 1)
                if slot(b, j) in RANK:
                    gate_exp(RANK[slot(b, j)])
                if b + 1 < BATCH and j in XAT:
                    x_part(b + 1, XAT.index(j))
                if b + 1 < BATCH and j == ZAT:
                    bu_out(b + 1)

        @block.vector
        def _(dve):
            def value(c, g):
                dve.wait_ge(raised, c * G + g + 1)
                v = val[:, turn(c, g)]
                nc.vector.tensor_scalar(v, v, width[:, g:g + 1], unshift[:, g:g + 1], ALU.min, ALU.add).then_inc(valued, 1)

            def mask(c, g):
                if g == 1:
                    dve.wait_ge(abs_made, c + 1)
                    if c:
                        dve.wait_ge(merged, c * (G - 1))
                elif g >= 3:
                    dve.wait_ge(merged, c * (G - 1) + g - 2)
                nc.vector.tensor_scalar(inside[:, g % 2], absx, thr[:, g - 1:g], None, ALU.is_le).then_inc(masked, 1)

            def merge(c, g):
                dve.wait_ge(valued, c * G + g + 1)
                dve.wait_ge(masked, c * (G - 1) + g)
                if g >= 2:
                    dve.wait_ge(merged, c * (G - 1) + g - 1)
                nc.vector.copy_predicated(val[:, acc(c)], inside[:, g % 2], val[:, turn(c, g)]).then_inc(merged, 1)

            def finish(c):
                dve.wait_ge(merged, (c + 1) * (G - 1))
                nc.vector.scalar_tensor_tensor(val[:, acc(c)], absx, thr[:, G - 1:G], val[:, acc(c)],
                                               ALU.is_gt, ALU.mult).then_inc(q_made, 1)

            def quant(c, g):
                value(c, g)
                if g == 1:
                    mask(c, 1)
                if g and g + 1 < G:
                    mask(c, g + 1)
                if g:
                    merge(c, g)
                if g + 1 == G:
                    finish(c)

            def weight_lo(n):
                dve.wait_ge(w_hi_made, n + 1)
                if n >= 2:
                    dve.wait_ge(ofull, n - 1)
                nc.vector.tensor_tensor(w_lo[n % 2], wst[n % 2], w_hi[n % 2].bitcast(F32), ALU.subtract).then_inc(w_lo_made, 1)

            def k_add(h, o):
                dve.wait_ge(k_in, 16 * (h + 1))
                dve.wait_ge(kfull, h * KT + o + 1)
                update = zbank if h else sbank[o % 2]
                nc.vector.tensor_tensor(kst[:, o], update, kst[:, o], ALU.add).then_inc(k_sum, 1)

            def kp_lo_part(h):
                for o in range(KT):
                    dve.wait_ge(kp_hi_made, h * KT + o + 1)
                    nc.vector.tensor_tensor(kp_lo[:, o], kst[:, o], kp_hi[:, o].bitcast(F32), ALU.subtract).then_inc(kp_lo_made, 1)

            dve.wait_ge(par_in, 16)
            nc.vector.max(thr, par[:, 0])
            nc.vector.reciprocal(inv, par[:, 1])
            nc.vector.tensor_scalar(width, par[:, 1], LEVELS, None, ALU.mult)
            nc.vector.tensor_tensor(shift, par[:, 1], par[:, 2], ALU.mult).then_inc(table_step, 1)
            dve.wait_ge(table_step, 1)
            nc.vector.tensor_scalar(unshift, shift, -1.0, None, ALU.mult).then_inc(tables, 1)
            dve.wait_ge(mix_in, 32)
            nc.vector.tensor_tensor(gmix, gate_rep.unsqueeze(1).to_broadcast([P, RG, BATCH]),
                                    gsel.unsqueeze(2).to_broadcast([P, RG, BATCH]), ALU.mult).then_inc(gmix_made, 1)
            nc.vector.memset(mg[:, :, 0:ER], 0.0).then_inc(mg_zeroed, 1)
            GATE_STEPS = 10
            def then(ins, n):
                ins.then_inc(gate_step, 1)
                dve.wait_ge(gate_step, n)

            def order(c):
                n = c * GATE_STEPS
                mid = midbank[:, 0:TT * RT].rearrange("p (t m) -> p t m", t=TT)
                dve.wait_ge(mid_made, c + 1)
                then(nc.vector.tensor_copy(lg, mid[:, :, ER:RT]), n + 1)
                then(nc.vector.reduce_max(best, lg, AX), n + 2)
                nc.vector.tensor_tensor(gap, lg, best.unsqueeze(2).to_broadcast([P, TT, E]), ALU.subtract).then_inc(gap_made, 1)
                mine = lg.unsqueeze(3).to_broadcast([P, TT, E, E])
                other = lg.unsqueeze(2).to_broadcast([P, TT, E, E])
                then(nc.vector.tensor_tensor(ties, other, mine, ALU.is_equal), n + 3)
                then(nc.vector.tensor_tensor(ties, ties, before, ALU.mult), n + 4)
                then(nc.vector.tensor_tensor(beats, other, mine, ALU.is_gt), n + 5)
                then(nc.vector.tensor_tensor(beats, beats, ties, ALU.add), n + 6)
                then(nc.vector.reduce_sum(rank, beats, AX), n + 7)

            def gate(c):
                n = c * GATE_STEPS
                mid = midbank[:, 0:TT * RT].rearrange("p (t m) -> p t m", t=TT)
                dve.wait_ge(exp_made, c + 1)
                then(nc.vector.scalar_tensor_tensor(gates, rank, TOP_K, expo, ALU.is_lt, ALU.mult), n + 8)
                then(nc.vector.reduce_sum(total, gates, AX), n + 9)
                then(nc.vector.reciprocal(total, total), n + 10)
                nc.vector.scalar_tensor_tensor(gates, gates, LORA0, total.unsqueeze(2).to_broadcast([P, TT, E]),
                                               ALU.mult, ALU.mult).then_inc(gates_made, 1)
                dve.wait_ge(gates_made, c + 1)
                nc.vector.tensor_tensor(mg[:, :, ER:2 * ER].rearrange("p t (e r) -> p t e r", e=E), mid[:, :, 0:ER].rearrange("p t (e r) -> p t e r", e=E),
                                        gates.unsqueeze(3).to_broadcast([P, TT, E, R0]), ALU.mult).then_inc(mg_made, 1)

            def x_part(c, p):
                dve.wait_ge(x_hi_made, c * XPARTS + p + 1)
                part = slice(p * XK, (p + 1) * XK)
                nc.vector.tensor_tensor(x_lo[:, c % 2, part], xbuf[:, c % 2, part], x_hi[:, c % 2, part].bitcast(F32),
                                        ALU.subtract).then_inc(x_lo_made, 1)

            quant(*ORDER[0])
            for o in range(KT):
                k_add(0, o)
            kp_lo_part(0)
            weight_lo(0)
            quant(*ORDER[1])
            quant(*ORDER[2])
            dve.wait_ge(cfull, 1)
            dve.wait_ge(consts_in, 16 * N_CONST)
            for q in range(BATCH // BG):
                last = nc.vector.scalar_tensor_tensor(cbd[:, q], cbank[:, q * P:(q + 1) * P], LORA1, bdmask, ALU.mult, ALU.mult)
            last.then_inc(cbd_made, 1)
            weight_lo(1)
            for i in range(3, AHEAD):
                quant(*ORDER[i])
            def ranks(k):
                if k in RANK:
                    order(RANK[k])
                if k in GATE:
                    gate(GATE[k])

            def p_out(n):
                dve.wait_ge(p_hi_made, n + 1)
                h, i = divmod(n, KT)
                nc.vector.tensor_tensor(p_lo[:, h, i], obank[n % RING], p_hi[:, h, i].bitcast(F32), ALU.subtract).then_inc(ofree, 1)

            for n in range(STEPS):
                if 0 < n < KT:
                    k_add(1, n - 1)
                if n == KT:
                    kp_lo_part(1)
                if n and n + 1 < STEPS:
                    weight_lo(n + 1)
                if n:
                    p_out(n - 1)
                if n == KT - 1:
                    k_add(1, n)
                for c, g in GROUPS[n]:
                    quant(c, g)
                ranks(n)
            dve.wait_ge(bet_hi_made, 1)
            nc.vector.tensor_tensor(bet_lo, bet, bet_hi.bitcast(F32), ALU.subtract).then_inc(bet_lo_made, 1)
            p_out(STEPS - 1)
            for p in range(XPARTS):
                x_part(0, p)
            for b in range(BATCH):
                for j in range(KT):
                    ranks(slot(b, j))
                    for c, g in GROUPS[slot(b, j)]:
                        quant(c, g)
                    if b + 1 < BATCH and j - 1 in XAT:
                        x_part(b + 1, XAT.index(j - 1))

        @block.tensor
        def _(pe):
            mm = nc.tensor.matmul
            gm = gmix.rearrange("p r b -> p (r b)")
            pe.wait_ge(gmix_made, 1)
            def k_update(h, o):
                if h:
                    pe.wait_ge(k_in, 32)
                    pe.wait_ge(v_made, 1)
                    pe.wait_ge(k_sum, KT + o)
                elif o >= 2:
                    pe.wait_ge(k_sum, o - 1)
                mm(zbank if h else sbank[o % 2], tst[2 * R:3 * R, 0, o * P:(o + 1) * P], tst[2 * R:3 * R, 1, h * HALF:(h + 1) * HALF],
                   start=True, stop=True).then_inc(kfull, 1)

            def v_product(h):
                pe.wait_ge(k_sum, (h + 1) * KT)
                if h == 0:
                    pe.wait_ge(bw_in, 16)
                else:
                    pe.wait_ge(v_made, 1)
                for o in range(KT):
                    last = mm(misc, bw[:, o], kst[:, o], start=o == 0, stop=o == KT - 1)
                last.then_inc(vfull, 1)

            for g in range(NG):
                pe.wait_ge(lora_in[g], 16)
                for o in range(KT):
                    at = o % 2 * BATCH * R + g * BATCH * RG
                    last = mm(obank[o // 2][:, at:at + BATCH * RG], la[:, g, o * P:(o + 1) * P], gm, start=True, stop=True)
                    if g == NG - 1 and o % 2:
                        last.then_inc(afull, 1)
            pe.wait_ge(shared_in, 32)
            pe.wait_ge(k_in, 16)
            for o in range(KT):
                k_update(0, o)
            v_product(0)
            pe.wait_ge(bw_in, 16)
            pe.wait_ge(afree, KT // 2)
            for o in range(KT):
                last = mm(cbank[:, 0:BATCH * R], bw[:, o], aefft[:, o], start=o == 0, stop=o == KT - 1)
            last.then_inc(cfull, 1)
            pe.wait_ge(lb_in, 16)
            for n in range(NG * HALVES):
                g, h = divmod(n, HALVES)
                if n >= RING:
                    pe.wait_ge(t_made, n - RING + 1)
                mm(obank[n % RING][0:2 * R], gm, lb[:, g, h * HALF:(h + 1) * HALF], start=True, stop=True).then_inc(tfull, 1)
            def mid(c):
                pe.wait_ge(q_made, c + 1)
                pe.wait_ge(ra_in, 16)
                if c:
                    pe.wait_ge(mgt_made, c)
                for t in range(TT):
                    for k in range(KT):
                        last = mm(midbank[:, t * RT:(t + 1) * RT], val[:, acc(c), k, t * P:(t + 1) * P], ra[:, k],
                                  start=k == 0, stop=k == KT - 1)
                last.then_inc(mid_made, 1)

            def gated_turn(c):
                pe.wait_ge(mg_made, c + 1)
                if c == 0:
                    pe.wait_ge(mg_zeroed, 1)
                for t in range(TT):
                    last = mm(mgbank[:, t * P:(t + 1) * P], mg[:, t], ident.bitcast(F32), start=True, stop=True)
                last.then_inc(mgt_full, 1)

            def z_begin(c):
                t = c % 2
                pe.wait_ge(ub_in[t], 32 * (c // 2 + 1))
                pe.wait_ge(bet_in, 16)
                if c:
                    pe.wait_ge(zt_made, c)
                    pe.wait_ge(bu_made, c)
                for k in range(KT):
                    last = mm(zbank[ER:2 * ER, TOK:TOK + 2 * R], bet[:, k, ER:2 * ER], ub[:, t, k], start=k == 0, stop=k == KT - 1)
                last.then_inc(bufull, 1)
                pe.wait_ge(xbuf_in[t], 16 + 32 * (c // 2))
                for k in range(KT):
                    mm(zbank[0:2 * R, 0:TOK], ub[:, t, k], xbuf[:, t, k], start=k == 0, stop=False)

            def z_end(c):
                pe.wait_ge(bu_made, c + 1)
                pe.wait_ge(mgt_made, c + 1)
                mm(zbank[0:2 * R, 0:TOK], bu[2 * R:P, c % 2], zt[2 * R:P, c % ZSLOTS], start=False, stop=True).then_inc(zfull, 1)

            pe.wait_ge(ident_made, 1)
            pe.wait_ge(alt_in, 16 * BATCH)
            pe.wait_ge(cbd_made, 1)
            for n in range(STEPS):
                h, i = divmod(n, KT)
                if h == 0:
                    pe.wait_ge(w_in[n % 2], 16 * (n // 2 + 1))
                    if i < 2:
                        pe.wait_ge(k_sum, KT - 1 + i)
                    else:
                        pe.wait_ge(u_made, i - 1)
                    for o in range(KT):
                        mm(sbank[i % 2][:, 0:BATCH * R], wst[n % 2][:, o], aefft[:, o], start=o == 0, stop=False)
                    for q in range(BATCH // BG):
                        last = mm(sbank[i % 2][:, q * P:(q + 1) * P], alt[:, q, i * P:(i + 1) * P], cbd[:, q],
                                  start=False, stop=q == BATCH // BG - 1)
                    last.then_inc(ufull, 1)
                    if n == KT - 1:
                        k_update(1, n)
                    if n in MID:
                        mid(MID[n])
                pe.wait_ge(w_lo_made, n + 1)
                if n < RING:
                    pe.wait_ge(t_made, NG * HALVES - RING + 1 + n)
                else:
                    pe.wait_ge(ofree, n - RING + 1)
                for o in range(KT):
                    if i == 0:
                        pe.wait_ge(kp_lo_made, h * KT + o + 1)
                    mm(obank[n % RING], w_hi[n % 2][:, o], kp_hi[:, o], start=o == 0, stop=False)
                    mm(obank[n % RING], w_hi[n % 2][:, o], kp_lo[:, o], start=False, stop=False)
                    if o == 0 and i * P // HALF == h:
                        mm(obank[n % RING][:, i * P % HALF:i * P % HALF + P], ident, ident, start=False, stop=False)
                    last = mm(obank[n % RING], w_lo[n % 2][:, o], kp_hi[:, o], start=False, stop=o == KT - 1)
                last.then_inc(ofull, 1)
                if n < KT - 1:
                    k_update(1, n)
                if n == KT - 1:
                    v_product(1)
                if n in MID and h:
                    mid(MID[n])
                if n in TURN:
                    gated_turn(TURN[n])
            z_begin(0)
            pe.wait_ge(bet_lo_made, 1)
            pe.wait_ge(k_sum, HALVES * KT)
            for h in range(HALVES):
                for k in range(KT):
                    pe.wait_ge(ofree, h * KT + k + 1)
                    mm(sbank[h], bet_hi[:, k], p_hi[:, h, k], start=k == 0, stop=False)
                    mm(sbank[h], bet_hi[:, k], p_lo[:, h, k], start=False, stop=False)
                    last = mm(sbank[h], bet_lo[:, k], p_hi[:, h, k], start=False, stop=k == KT - 1)
                last.then_inc(bpfull, 1)
            z_end(0)

            for b in range(BATCH):
                s = b % 2
                pe.wait_ge(x_lo_made, (b + 1) * XPARTS)
                for j in range(KT):
                    h, at = j // (KT // 2), j % (KT // 2) * P
                    q = b * KT + j
                    if q < RING:
                        pe.wait_ge(ofree, STEPS)
                    elif q < CRING:
                        pe.wait_ge(bp_made, 2 * HALVES)
                    else:
                        pe.wait_ge(ofree, STEPS + q - CRING + 1)
                    o = cols[q % CRING][:, 0:TOK]
                    for k in range(KT):
                        mm(o, p_hi[:, h, k, at:at + P], x_hi[:, s, k], start=k == 0, stop=False)
                        mm(o, p_hi[:, h, k, at:at + P], x_lo[:, s, k], start=False, stop=False)
                        mm(o, p_lo[:, h, k, at:at + P], x_hi[:, s, k], start=False, stop=False)
                    if j == CLOSE[b]:
                        if j:
                            z_end(b)
                        pe.wait_ge(zt_made, b + 1)
                        pe.wait_ge(tb_in[s], 16 * (b // 2 + 1))
                        pe.wait_ge(v_moved, 32)
                        pe.wait_ge(bp_made, HALVES * min(b + 1, 2))
                    for m in range(CLOSE[b] + 1) if j == CLOSE[b] else [j] if j > CLOSE[b] else []:
                        mm(cols[(b * KT + m) % CRING][:, 0:TOK], tb[:, s, m * P:(m + 1) * P], zt[:, b % ZSLOTS], start=False, stop=True).then_inc(ofull, 1)
                    if slot(b, j) in MID:
                        mid(MID[slot(b, j)])
                    if slot(b, j) in TURN:
                        gated_turn(TURN[slot(b, j)])
                    if b + 1 < BATCH and j == ZAT:
                        z_begin(b + 1)
                if b + 1 < BATCH and CLOSE[b + 1] == 0:
                    z_end(b + 1)


def kernel(**inputs):
    import concourse.bacc as bacc
    from concourse.bass_utils import run_bass_kernel_spmd

    v = {k: np.asarray(x) for k, x in inputs.items()}
    c = np.ascontiguousarray
    i4, i16 = np.arange(E), np.arange(P)
    before = np.broadcast_to((i4[None, :] < i4[:, None]).astype(np.float32), (P, TT, E, E))
    arrays = {
        "xt": c(v["x"].reshape(BATCH * TOK, D).T),
        "par": c(np.broadcast_to(np.stack([v["condB_thresholds"], v["condB_deltas"], v["condB_zeropoints"]]), (P, 3, G))),
        "ra": c(np.concatenate([v["L0_ffn_A"].reshape(ER, D), v["L0_ffn_router_w"]]).reshape(RT, KT, P).transpose(2, 1, 0)),
        "bet": c(np.tile(v["L0_ffn_B"].reshape(E, KT, P, R0).transpose(2, 1, 0, 3).reshape(P, KT, ER), (1, 1, 2))),
        "w": c(v["L1_cond_W"]),
        "k": c(v["L1_ffn_kernel"]),
        "as": c(v["L1_ffn_lora_A_shared"]),
        "bst": c(v["L1_ffn_lora_B_shared"].T),
        "la": c(v["L1_ffn_lora_A"].transpose(1, 0, 2).reshape(NG, P, D).transpose(1, 0, 2)),
        "lb": c(v["L1_ffn_lora_B"].transpose(2, 0, 1).reshape(NG, P, D).transpose(1, 0, 2)),
        "gate_rep": c(np.tile(v["L1_ffn_gate"].T, (RG, 1))),
        "bw": c(np.tile(v["L1_cond_lora_B_w"].reshape(KT, P, R).transpose(1, 0, 2), (1, 1, BG))),
        "al": c(v["L1_cond_lora_A"].reshape(LAB, KT, P, R).transpose(0, 2, 1, 3)),
        "alt": c(v["L1_cond_lora_A"].transpose(0, 2, 1)),
        "bias": c(v["L1_ffn_bias"].reshape(KT, P).T),
        "gsel": (i16[:, None] // NL == np.arange(RG)[None, :]).astype(np.float32),
        "bdmask": (i16[:, None] // R == i16[None, :] // R).astype(np.float32),
        "ident": np.eye(P, dtype=np.float32),
        "before": c(before),
        "itok": c(v["itok_B_0_2"].reshape(1, BATCH)),
    }
    nc = bacc.Bacc("TRN2", target_bir_lowering=False, num_devices=1)
    aps = {k: nc.dram_tensor(f"{k}_in", x.shape, mybir.dt.from_np(x.dtype), kind="ExternalInput").ap() for k, x in arrays.items()}
    out_t = nc.dram_tensor("out_t", (D, BATCH * TOK), F32, kind="ExternalOutput").ap()
    itok = aps.pop("itok")
    build(nc, aps, out_t, itok)
    r = run_bass_kernel_spmd(nc, [{f"{k}_in": x for k, x in arrays.items()}], core_ids=[0])
    return c(r.results[0]["out_t"].T).reshape(BATCH, TOK, D)
```
